# Optimizing a Trainium2 kernel written in Bass

```python
import numpy as np
import jax
import jax.numpy as jnp

def _softmax(x, axis=-1):
    return jax.nn.softmax(x, axis=axis)

def _gelu(x):
    return jax.nn.gelu(x, approximate=True)

def _silu(x):
    return jax.nn.silu(x)

def _sigmoid(x):
    return jax.nn.sigmoid(x)

def _layernorm(x, axis=-1, eps=1e-05):
    m = jnp.mean(x, axis=axis, keepdims=True)
    v = jnp.var(x, axis=axis, keepdims=True)
    return (x - m) / jnp.sqrt(v + eps)

def _scatter_add(tgt, idx, src, axis=0):
    return tgt.at[idx].add(src)

def _segment_sum(src, seg, n):
    return jax.ops.segment_sum(src, seg, n)
kernel_name = 'mk_decoder_preln_d2_seqx_r4_496691'

def setup_inputs(seed: int=0):
    np.random.seed(seed)
    _w = jnp.asarray

    def _rec_inputs():
        import jax
        import jax.numpy as jnp
        _rk = jax.random.key(seed)
        x = -0.0002928 + 1 * jax.random.normal(jax.random.fold_in(_rk, 1), (8, 256, 256), jnp.float32)
        _lenS = 256 - jax.random.randint(jax.random.fold_in(_rk, 7), (8,), 0, max(1, 256 // 4) + 1, jnp.int32)
        _lenS2 = 256 - jax.random.randint(jax.random.fold_in(_rk, 8), (8,), 0, max(1, 256 // 4) + 1, jnp.int32)
        _ctx_1024P = jax.random.normal(jax.random.fold_in(_rk, 11), (8, 16, 256), jnp.float32)
        _ctx_1024c = jax.random.dirichlet(jax.random.fold_in(_rk, 511), 0.3 * jnp.ones((16,), jnp.float32), (8, 256))
        _ctx_1024t = jnp.einsum('bsk,bkd->bsd', _ctx_1024c, _ctx_1024P)
        _ctx_1024t = _ctx_1024t * jax.lax.rsqrt(jnp.mean(jnp.square(_ctx_1024t)) + 1e-12) * 0.953939
        ctx_1024 = -1.39393e-06 + 0.999914 * (_ctx_1024t + 0.3 * jax.random.normal(jax.random.fold_in(_rk, 611), (8, 256, 256), jnp.float32))
        _validS = jnp.arange(256)[None, :] < _lenS[:, None]
        _validS2 = jnp.arange(256)[None, :] < _lenS2[:, None]
        _causal = jnp.tril(jnp.ones((256, 256), dtype=bool))
        mask_SxS2_bk1 = jnp.broadcast_to(_validS2[0:1, :], (256, 256))
        return (x, ctx_1024, mask_SxS2_bk1)
    x, ctx_1024, mask_SxS2_bk1 = _rec_inputs()

    def _L0_attn_setup():
        import jax, jax.numpy as jnp
        import numpy as np
        D_MODEL = 256
        NUM_HEADS = 16
        HEAD_DIM = D_MODEL // NUM_HEADS
        LN_EPS = 0.001
        key = jax.random.key(seed)
        ks = jax.random.split(key, 10)
        B, T = (2, 512)
        s = 1.0 / np.sqrt(D_MODEL)
        return {'x': jax.random.normal(ks[0], (B, T, D_MODEL), dtype=jnp.float32), 'Wq': jax.random.normal(ks[1], (D_MODEL, D_MODEL), dtype=jnp.float32) * s, 'Wk': jax.random.normal(ks[2], (D_MODEL, D_MODEL), dtype=jnp.float32) * s, 'Wv': jax.random.normal(ks[3], (D_MODEL, D_MODEL), dtype=jnp.float32) * s, 'Wg': jax.random.normal(ks[4], (D_MODEL, D_MODEL), dtype=jnp.float32) * s, 'bg': jnp.zeros((D_MODEL,), dtype=jnp.float32), 'Wo': jax.random.normal(ks[5], (D_MODEL, D_MODEL), dtype=jnp.float32) * s, 'bo': jnp.zeros((D_MODEL,), dtype=jnp.float32), 'ln_gamma': jnp.ones((D_MODEL,), dtype=jnp.float32), 'ln_beta': jnp.zeros((D_MODEL,), dtype=jnp.float32)}
    _L0_attn_all = _L0_attn_setup()
    _L0_attn_in = {k: v for k, v in _L0_attn_all.items() if k in ('Wq', 'Wk', 'Wv', 'Wg', 'bg', 'Wo', 'bo', 'ln_gamma', 'ln_beta')}
    del _L0_attn_all

    def _L0_xattn_setup():
        import jax, jax.numpy as jnp
        import numpy as np
        B, S, E, H = (2, 512, 256, 16)
        DK = E // H
        key = jax.random.key(seed)
        ks = jax.random.split(key, 8)
        scale = 1.0 / np.sqrt(E)
        inp = {'query': jax.random.normal(ks[0], (B, S, E), jnp.float32), 'key': jax.random.normal(ks[1], (B, S, E), jnp.float32), 'value': jax.random.normal(ks[2], (B, S, E), jnp.float32), 'attn_mask': jnp.triu(jnp.ones((S, S), jnp.bool_), k=1), 'Wq': jax.random.normal(ks[3], (E, E), jnp.float32) * scale, 'bq': jnp.zeros((E,), jnp.float32), 'Wk': jax.random.normal(ks[4], (E, E), jnp.float32) * scale, 'bk': jnp.zeros((E,), jnp.float32), 'Wv': jax.random.normal(ks[5], (E, E), jnp.float32) * scale, 'bv': jnp.zeros((E,), jnp.float32), 'Wo': jax.random.normal(ks[6], (E, E), jnp.float32) * scale, 'bo': jnp.zeros((E,), jnp.float32)}
        return inp
    _L0_xattn_all = _L0_xattn_setup()
    _L0_xattn_in = {k: v for k, v in _L0_xattn_all.items() if k in ('Wq', 'bq', 'Wk', 'bk', 'Wv', 'bv', 'Wo', 'bo')}
    del _L0_xattn_all

    def _L0_ffn_setup():
        import jax, jax.numpy as jnp
        import numpy as np
        DIM = 256
        HIDDEN = 1024
        E = 8
        B, S = (2, 1024)
        key = jax.random.key(seed)
        ks = jax.random.split(key, 8)
        sd = 1.0 / np.sqrt(DIM)
        sh = 1.0 / np.sqrt(HIDDEN)
        return {'x': jax.random.normal(ks[0], (B, S, DIM), dtype=jnp.float32), 'router_w': jax.random.uniform(ks[1], (DIM, E), jnp.float32, -sd, sd), 'router_b': jax.random.uniform(ks[2], (E,), jnp.float32, -sd, sd), 'w1': jax.random.uniform(ks[3], (E, DIM, 2 * HIDDEN), jnp.float32, -sd, sd), 'b1': jax.random.uniform(ks[4], (E, 2 * HIDDEN), jnp.float32, -sd, sd), 'w2': jax.random.uniform(ks[5], (E, HIDDEN, DIM), jnp.float32, -sh, sh), 'b2': jax.random.uniform(ks[6], (E, DIM), jnp.float32, -sh, sh)}
    _L0_ffn_all = _L0_ffn_setup()
    _L0_ffn_in = {k: v for k, v in _L0_ffn_all.items() if k in ('router_w', 'router_b', 'w1', 'b1', 'w2', 'b2')}
    del _L0_ffn_all

    def _L1_attn_setup():
        import jax, jax.numpy as jnp
        import numpy as np
        HEADS = 16
        DIM_HEAD = 64
        B, T, C = (4, 512, 256)

        def apply_rope(x):
            d = x.shape[-1]
            seq_len = x.shape[1]
            inv_freq = 1.0 / 10000.0 ** (jnp.arange(0, d, 2, dtype=jnp.float32) / d)
            pos = jnp.arange(seq_len, dtype=jnp.float32)
            ang = pos[:, None] * inv_freq[None, :]
            sin = jnp.sin(ang)[None]
            cos = jnp.cos(ang)[None]
            x1, x2 = (x[..., 0::2], x[..., 1::2])
            rot = jnp.stack([x1 * cos - x2 * sin, x1 * sin + x2 * cos], axis=-1)
            return rot.reshape(x.shape)
        key = jax.random.key(seed)
        ks = jax.random.split(key, 6)
        inner = HEADS * DIM_HEAD
        w = 0.02
        return {'x': jax.random.normal(ks[0], (B, T, C), dtype=jnp.float32), 'Wq': jax.random.normal(ks[1], (C, inner), dtype=jnp.float32) * w, 'Wk': jax.random.normal(ks[2], (C, inner), dtype=jnp.float32) * w, 'Wv': jax.random.normal(ks[3], (C, inner), dtype=jnp.float32) * w, 'Wo': jax.random.normal(ks[4], (inner, C), dtype=jnp.float32) * w, 'bo': jnp.zeros((C,), dtype=jnp.float32)}
    _L1_attn_all = _L1_attn_setup()
    _L1_attn_in = {k: v for k, v in _L1_attn_all.items() if k in ('Wq', 'Wk', 'Wv', 'Wo', 'bo')}
    del _L1_attn_all

    def _L1_xattn_setup():
        import jax, jax.numpy as jnp
        import numpy as np
        D_MODEL = 256
        N_HEAD = 16

        def _split(t, n_head):
            B, L, D = t.shape
            return t.reshape(B, L, n_head, D // n_head).transpose(0, 2, 1, 3)
        key = jax.random.key(seed)
        ks = jax.random.split(key, 12)
        B, L, D = (4, 512, D_MODEL)
        s = 1.0 / np.sqrt(D)
        inp = {'q': jax.random.normal(ks[0], (B, L, D), jnp.float32), 'k': jax.random.normal(ks[1], (B, L, D), jnp.float32), 'v': jax.random.normal(ks[2], (B, L, D), jnp.float32), 'w_q': jax.random.normal(ks[3], (D, D), jnp.float32) * s, 'b_q': jnp.zeros((D,), jnp.float32), 'w_k': jax.random.normal(ks[4], (D, D), jnp.float32) * s, 'b_k': jnp.zeros((D,), jnp.float32), 'w_v': jax.random.normal(ks[5], (D, D), jnp.float32) * s, 'b_v': jnp.zeros((D,), jnp.float32), 'w_o': jax.random.normal(ks[6], (D, D), jnp.float32) * s, 'b_o': jnp.zeros((D,), jnp.float32)}
        return inp
    _L1_xattn_all = _L1_xattn_setup()
    _L1_xattn_in = {k: v for k, v in _L1_xattn_all.items() if k in ('w_q', 'b_q', 'w_k', 'b_k', 'w_v', 'b_v', 'w_o', 'b_o')}
    del _L1_xattn_all

    def _L1_ffn_setup():
        import jax, jax.numpy as jnp
        import numpy as np
        NUM_EXPERTS = 8
        TOP_K = 2
        B, T, D, F = (4, 512, 256, 704)
        key = jax.random.key(seed)
        ks = jax.random.split(key, 5)
        return {'x': jax.random.normal(ks[0], (B, T, D), dtype=jnp.float32), 'router_w': jax.random.normal(ks[1], (D, NUM_EXPERTS), dtype=jnp.float32) * 0.02, 'gate_proj': jax.random.normal(ks[2], (NUM_EXPERTS, D, F), dtype=jnp.float32) * 0.02, 'up_proj': jax.random.normal(ks[3], (NUM_EXPERTS, D, F), dtype=jnp.float32) * 0.02, 'down_proj': jax.random.normal(ks[4], (NUM_EXPERTS, F, D), dtype=jnp.float32) * 0.02}
    _L1_ffn_all = _L1_ffn_setup()
    _L1_ffn_in = {k: v for k, v in _L1_ffn_all.items() if k in ('router_w', 'gate_proj', 'up_proj', 'down_proj')}
    del _L1_ffn_all
    return {'x': x, 'ctx_1024': ctx_1024, 'mask_SxS2_bk1': mask_SxS2_bk1, 'L0_attn_Wq': _L0_attn_in['Wq'], 'L0_attn_Wk': _L0_attn_in['Wk'], 'L0_attn_Wv': _L0_attn_in['Wv'], 'L0_attn_Wg': _L0_attn_in['Wg'], 'L0_attn_bg': _L0_attn_in['bg'], 'L0_attn_Wo': _L0_attn_in['Wo'], 'L0_attn_bo': _L0_attn_in['bo'], 'L0_attn_ln_gamma': _L0_attn_in['ln_gamma'], 'L0_attn_ln_beta': _L0_attn_in['ln_beta'], 'L0_xattn_Wq': _L0_xattn_in['Wq'], 'L0_xattn_bq': _L0_xattn_in['bq'], 'L0_xattn_Wk': _L0_xattn_in['Wk'], 'L0_xattn_bk': _L0_xattn_in['bk'], 'L0_xattn_Wv': _L0_xattn_in['Wv'], 'L0_xattn_bv': _L0_xattn_in['bv'], 'L0_xattn_Wo': _L0_xattn_in['Wo'], 'L0_xattn_bo': _L0_xattn_in['bo'], 'L0_ffn_router_w': _L0_ffn_in['router_w'], 'L0_ffn_router_b': _L0_ffn_in['router_b'], 'L0_ffn_w1': _L0_ffn_in['w1'], 'L0_ffn_b1': _L0_ffn_in['b1'], 'L0_ffn_w2': _L0_ffn_in['w2'], 'L0_ffn_b2': _L0_ffn_in['b2'], 'L1_attn_Wq': _L1_attn_in['Wq'], 'L1_attn_Wk': _L1_attn_in['Wk'], 'L1_attn_Wv': _L1_attn_in['Wv'], 'L1_attn_Wo': _L1_attn_in['Wo'], 'L1_attn_bo': _L1_attn_in['bo'], 'L1_xattn_w_q': _L1_xattn_in['w_q'], 'L1_xattn_b_q': _L1_xattn_in['b_q'], 'L1_xattn_w_k': _L1_xattn_in['w_k'], 'L1_xattn_b_k': _L1_xattn_in['b_k'], 'L1_xattn_w_v': _L1_xattn_in['w_v'], 'L1_xattn_b_v': _L1_xattn_in['b_v'], 'L1_xattn_w_o': _L1_xattn_in['w_o'], 'L1_xattn_b_o': _L1_xattn_in['b_o'], 'L1_ffn_router_w': _L1_ffn_in['router_w'], 'L1_ffn_gate_proj': _L1_ffn_in['gate_proj'], 'L1_ffn_up_proj': _L1_ffn_in['up_proj'], 'L1_ffn_down_proj': _L1_ffn_in['down_proj']}

def reference(x, ctx_1024, mask_SxS2_bk1, L0_attn_Wq, L0_attn_Wk, L0_attn_Wv, L0_attn_Wg, L0_attn_bg, L0_attn_Wo, L0_attn_bo, L0_attn_ln_gamma, L0_attn_ln_beta, L0_xattn_Wq, L0_xattn_bq, L0_xattn_Wk, L0_xattn_bk, L0_xattn_Wv, L0_xattn_bv, L0_xattn_Wo, L0_xattn_bo, L0_ffn_router_w, L0_ffn_router_b, L0_ffn_w1, L0_ffn_b1, L0_ffn_w2, L0_ffn_b2, L1_attn_Wq, L1_attn_Wk, L1_attn_Wv, L1_attn_Wo, L1_attn_bo, L1_xattn_w_q, L1_xattn_b_q, L1_xattn_w_k, L1_xattn_b_k, L1_xattn_w_v, L1_xattn_b_v, L1_xattn_w_o, L1_xattn_b_o, L1_ffn_router_w, L1_ffn_gate_proj, L1_ffn_up_proj, L1_ffn_down_proj):
    import jax
    import jax.numpy as jnp

    def _L0_attn_ref(x, Wq, Wk, Wv, Wg, bg, Wo, bo, ln_gamma, ln_beta):
        import jax, jax.numpy as jnp
        import numpy as np
        D_MODEL = 256
        NUM_HEADS = 16
        HEAD_DIM = D_MODEL // NUM_HEADS
        LN_EPS = 0.001
        B, T, D = x.shape
        H, dh = (NUM_HEADS, HEAD_DIM)

        def split_heads(z):
            return z.reshape(B, T, H, dh).transpose(0, 2, 1, 3)
        Q = split_heads(x @ Wq)
        K = split_heads(x @ Wk)
        V = split_heads(x @ Wv)
        G = jax.nn.swish(x @ Wg + bg)
        idx = jnp.arange(T, dtype=jnp.float32)
        diff = idx[:, None] - idx[None, :]
        causal = (diff >= 0).astype(jnp.float32)
        gammas = 1.0 - 2.0 ** (-5.0 - jnp.arange(H, dtype=jnp.float32))
        Dmask = gammas[:, None, None] ** jnp.maximum(diff, 0.0) * causal
        scale = float(dh) ** 0.5
        scores = jnp.einsum('bhtd,bhsd->bhts', Q, K) / scale
        ret = jnp.einsum('bhts,bhsd->bhtd', scores * Dmask[None], V)
        ret = ret.transpose(0, 2, 1, 3).reshape(B, T, D)
        mu = jnp.mean(ret, axis=-1, keepdims=True)
        var = jnp.mean(jnp.square(ret - mu), axis=-1, keepdims=True)
        ln = (ret - mu) / jnp.sqrt(var + LN_EPS) * ln_gamma + ln_beta
        return ln * G @ Wo + bo

    def _L0_xattn_ref(query, key, value, attn_mask, Wq, bq, Wk, bk, Wv, bv, Wo, bo):
        import jax, jax.numpy as jnp
        import numpy as np
        B, S, E, H = (2, 512, 256, 16)
        DK = E // H
        bs = query.shape[0]

        def proj(x, W, b):
            y = jnp.einsum('bse,ef->bsf', x, W) + b
            return y.reshape(bs, -1, H, DK).transpose(0, 2, 1, 3)
        q = proj(query, Wq, bq)
        k = proj(key, Wk, bk)
        v = proj(value, Wv, bv)
        scores = jnp.einsum('bhqd,bhkd->bhqk', q, k) / np.sqrt(DK).astype(jnp.float32)
        scores = jnp.where(attn_mask[None, None, :, :], jnp.float32(-1000000000.0), scores)
        attn = jax.nn.softmax(scores, axis=-1)
        ctx = jnp.einsum('bhqk,bhkd->bhqd', attn, v)
        concat = ctx.transpose(0, 2, 1, 3).reshape(bs, -1, E)
        return jnp.einsum('bse,ef->bsf', concat, Wo) + bo

    def _L0_ffn_ref(x, router_w, router_b, w1, b1, w2, b2):
        import jax, jax.numpy as jnp
        import numpy as np
        DIM = 256
        HIDDEN = 1024
        E = 8
        B, S = (2, 1024)
        logits = jnp.einsum('bsd,de->bse', x, router_w) + router_b
        probs = jax.nn.softmax(logits, axis=-1)
        top1 = jnp.argmax(probs, axis=-1)
        out = jnp.zeros_like(x)
        for i in range(E):
            h = jnp.einsum('bsd,df->bsf', x, w1[i]) + b1[i]
            a, g = jnp.split(h, 2, axis=-1)
            y = jnp.einsum('bsh,hd->bsd', a * jax.nn.sigmoid(g), w2[i]) + b2[i]
            out = out + jnp.where((top1 == i)[..., None], y, 0.0)
        return out

    def _L1_attn_ref(x, Wq, Wk, Wv, Wo, bo):
        import jax, jax.numpy as jnp
        import numpy as np
        HEADS = 16
        DIM_HEAD = 64
        B, T, C = (4, 512, 256)

        def apply_rope(x):
            d = x.shape[-1]
            seq_len = x.shape[1]
            inv_freq = 1.0 / 10000.0 ** (jnp.arange(0, d, 2, dtype=jnp.float32) / d)
            pos = jnp.arange(seq_len, dtype=jnp.float32)
            ang = pos[:, None] * inv_freq[None, :]
            sin = jnp.sin(ang)[None]
            cos = jnp.cos(ang)[None]
            x1, x2 = (x[..., 0::2], x[..., 1::2])
            rot = jnp.stack([x1 * cos - x2 * sin, x1 * sin + x2 * cos], axis=-1)
            return rot.reshape(x.shape)
        b, t, c = x.shape
        h, d = (HEADS, DIM_HEAD)
        scale = d ** (-0.5)

        def split_heads(z):
            return z.reshape(b, t, h, d).transpose(0, 2, 1, 3).reshape(b * h, t, d)
        q = split_heads(x @ Wq)
        k = split_heads(x @ Wk)
        v = split_heads(x @ Wv)
        q = apply_rope(q)
        k = apply_rope(k)
        sim = jnp.einsum('bid,bjd->bij', q, k) * scale
        causal = jnp.tril(jnp.ones((t, t), dtype=bool))
        sim = jnp.where(causal[None], sim, -jnp.inf)
        attn = jax.nn.softmax(sim, axis=-1)
        out = jnp.einsum('bij,bjd->bid', attn, v)
        out = out.reshape(b, h, t, d).transpose(0, 2, 1, 3).reshape(b, t, h * d)
        return out @ Wo + bo

    def _L1_xattn_ref(q, k, v, w_q, b_q, w_k, b_k, w_v, b_v, w_o, b_o):
        import jax, jax.numpy as jnp
        import numpy as np
        D_MODEL = 256
        N_HEAD = 16

        def _split(t, n_head):
            B, L, D = t.shape
            return t.reshape(B, L, n_head, D // n_head).transpose(0, 2, 1, 3)
        qp = q @ w_q.T + b_q
        kp = k @ w_k.T + b_k
        vp = v @ w_v.T + b_v
        qh, kh, vh = (_split(qp, N_HEAD), _split(kp, N_HEAD), _split(vp, N_HEAD))
        d_head = qh.shape[-1]
        score = jnp.einsum('bhqd,bhkd->bhqk', qh, kh) / jnp.sqrt(jnp.float32(d_head))
        attn = jax.nn.softmax(score, axis=-1)
        out = jnp.einsum('bhqk,bhkd->bhqd', attn, vh)
        B, H, L, d = out.shape
        out = out.transpose(0, 2, 1, 3).reshape(B, L, H * d)
        return out @ w_o.T + b_o

    def _L1_ffn_ref(x, router_w, gate_proj, up_proj, down_proj):
        import jax, jax.numpy as jnp
        import numpy as np
        NUM_EXPERTS = 8
        TOP_K = 2
        B, T, D, F = (4, 512, 256, 704)
        scores = jnp.einsum('btd,de->bte', x, router_w).astype(jnp.float32)
        probs = jax.nn.softmax(scores, axis=-1)
        routing_weights, routing_idx = jax.lax.top_k(probs, TOP_K)
        routing_weights = (routing_weights / jnp.sum(routing_weights, axis=-1, keepdims=True)).astype(x.dtype)
        one_hot = jax.nn.one_hot(routing_idx, NUM_EXPERTS, dtype=x.dtype)
        expert_w = jnp.einsum('btke,btk->bte', one_hot, routing_weights)
        dispatched = jnp.einsum('btd,btke->bted', x, one_hot)
        gate = jnp.einsum('bted,edf->btef', dispatched, gate_proj)
        up = jnp.einsum('bted,edf->btef', dispatched, up_proj)
        acts = jax.nn.silu(gate) * up
        expert_out = jnp.einsum('btef,efd->bted', acts, down_proj)
        return jnp.einsum('bted,bte->btd', expert_out, expert_w)
    x = x + _L0_attn_ref(_layernorm(x, axis=-1), L0_attn_Wq, L0_attn_Wk, L0_attn_Wv, L0_attn_Wg, L0_attn_bg, L0_attn_Wo, L0_attn_bo, L0_attn_ln_gamma, L0_attn_ln_beta)
    x = x + _L0_xattn_ref(_layernorm(x, axis=-1), ctx_1024, ctx_1024, mask_SxS2_bk1, L0_xattn_Wq, L0_xattn_bq, L0_xattn_Wk, L0_xattn_bk, L0_xattn_Wv, L0_xattn_bv, L0_xattn_Wo, L0_xattn_bo)
    x = x + _L0_ffn_ref(_layernorm(x, axis=-1), L0_ffn_router_w, L0_ffn_router_b, L0_ffn_w1, L0_ffn_b1, L0_ffn_w2, L0_ffn_b2)
    x = x + _L1_attn_ref(_layernorm(x, axis=-1), L1_attn_Wq, L1_attn_Wk, L1_attn_Wv, L1_attn_Wo, L1_attn_bo)
    x = x + _L1_xattn_ref(_layernorm(x, axis=-1), ctx_1024, ctx_1024, L1_xattn_w_q, L1_xattn_b_q, L1_xattn_w_k, L1_xattn_b_k, L1_xattn_w_v, L1_xattn_b_v, L1_xattn_w_o, L1_xattn_b_o)
    x = x + _L1_ffn_ref(_layernorm(x, axis=-1), L1_ffn_router_w, L1_ffn_gate_proj, L1_ffn_up_proj, L1_ffn_down_proj)
    return x

_drawn_inputs = setup_inputs


def setup_inputs(seed=0):
    import zlib

    import numpy as np

    out = dict(_drawn_inputs(seed))
    spreads = {'L0_attn_bg': (0.0, 0.1),
     'L0_attn_bo': (0.0, 0.1),
     'L0_attn_ln_gamma': (1.0, 0.2),
     'L0_attn_ln_beta': (0.0, 0.1),
     'L0_xattn_bq': (0.0, 0.1),
     'L0_xattn_bk': (0.0, 0.8),
     'L0_xattn_bv': (0.0, 0.1),
     'L0_xattn_bo': (0.0, 0.1),
     'L1_attn_bo': (0.0, 0.1),
     'L1_xattn_b_q': (0.0, 0.527),
     'L1_xattn_b_k': (0.0, 0.8),
     'L1_xattn_b_v': (0.0, 0.1),
     'L1_xattn_b_o': (0.0, 0.1)}
    factors = {'L0_ffn_b1': 7.288,
     'L0_ffn_b2': 4.4,
     'L1_attn_Wq': 8.0,
     'L1_attn_Wk': 8.0,
     'L1_ffn_router_w': 4.802,
     'L1_ffn_gate_proj': 4.167,
     'L1_ffn_up_proj': 4.125,
     'L1_ffn_down_proj': 4.131}
    for name, (base, spread) in spreads.items():
        noise = np.random.default_rng([zlib.crc32(name.encode()), seed]).standard_normal(out[name].shape)
        drawn = base * np.exp(spread * noise) if base else spread * noise
        out[name] = jnp.asarray(drawn.astype(out[name].dtype))
    for name, factor in factors.items():
        out[name] = (out[name] * factor).astype(out[name].dtype)
    return out
```

```python
import concourse.bass as bass
from concourse import mybir
from contextlib import ExitStack

F32 = mybir.dt.float32
BF16 = mybir.dt.bfloat16
U32 = mybir.dt.uint32
I32 = mybir.dt.int32
U8 = mybir.dt.uint8
ALU = mybir.AluOpType
ACT = mybir.ActivationFunctionType
AXX = mybir.AxisListType.X
ds = bass.ds

STAGES = 6
P = 128
BATCH = 8
SEQ = 256
DM = 256
TT = SEQ // P
DT = DM // P
TILES = BATCH * TT
HEADS = 16
NEG = -1.0e30
LN_EPS = 1e-5
RET_EPS = 1e-3
BANK = 512


def await_ge(eng, sem, value):
    if not (isinstance(value, int) and value <= 0):
        eng.wait_ge(sem, value)


def seq_steps(eng, step):
    step(0, 0, True, True, False)
    with eng.Fori(0, (BATCH - 2) // 2) as i:
        step(i * 2 + 1, 1, True, True, True)
        step(i * 2 + 2, 0, True, True, True)
    step(BATCH - 1, 1, False, True, True)
    step(BATCH, 0, False, False, True)


class Scope:

    taken = []

    def __init__(self, nc, ctx, name):
        self.nc, self.ctx, self.name = nc, ctx, name

    def sb(self, name, shape, dt=F32):
        return self.ctx.enter_context(self.nc.sbuf_tensor(f"{self.name}_{name}", shape, dt))

    def bank(self, name):
        return self.ctx.enter_context(self.nc.psum_tensor(f"{self.name}_{name}", [P, BANK], F32))

    def sem(self, name):
        s = self.nc.alloc_semaphore(f"{self.name}_{name}")
        Scope.taken.append(s)
        return s

    @staticmethod
    def clear_semaphores(nc):
        nc.all_engine_barrier()
        nc.clear_and_free_semaphores(list(Scope.taken))
        Scope.taken.clear()
        nc.all_engine_barrier()


def attention_layer(nc, name, x, consts, w, dh, cross, masked, causal):
    rope = not cross
    G = 16 if dh == 16 else 4
    NG = HEADS // G
    DI = HEADS * dh
    QTILES = 4 if dh == 16 else 8
    HPT = HEADS // QTILES
    PITCH = P // HPT
    SC = float(dh) ** -0.5
    ident, ident_bf = consts["ident"], consts["ident_bf"]

    if cross:
        USES = [("hT", 0, "act", 1), ("q", 0, "act", 2), ("q", 1, "act", 3), ("k", 0, "act", 4),
                ("k", 1, "act", 5), ("v", 0, "act", 6)]
    else:
        USES = [("hT", 0, "act", 1)]
        USES += [("qr", n, "dve", 2 + n) for n in range(4)]
        USES += [("kr", n, "dve", 6 + n) for n in range(4)]
        for n in range(4):
            USES += [("qT", n, "act", 10 + n), ("v", n, "act", 10 + n)]
        for n in range(4):
            USES += [("kT", n, "act", 14 + n // 2)]
    NF = len(USES)
    ACT_PER = {"hT": 1, "q": 2, "k": 2, "v": 1, "qT": 1, "kT": 1}
    DVE_PER = 3

    def emptied(b, j):
        e = USES[j][2]
        per = [(ACT_PER[u[0]] if e == "act" else DVE_PER) for u in USES if u[2] == e]
        upto = [(ACT_PER[u[0]] if e == "act" else DVE_PER) for u in USES[:j + 1] if u[2] == e]
        return e, b * sum(per) + sum(upto)

    with ExitStack() as ctx:
        sc = Scope(nc, ctx, name)
        sb, bank, sem = sc.sb, sc.bank, sc.sem
        WCOLS = QTILES * P
        wq = sb("wq", [P, DT, WCOLS])
        wk = sb("wk", [P, DT, WCOLS])
        wv = sb("wv", [P, DT, DI])
        wo = sb("wo", [P, DI // P, DM])
        bo = sb("bo", [P, DM])
        if cross:
            cT = [sb(f"cT{n}", [P, DT, SEQ]) for n in range(2)]
            bq = sb("bq", [P, QTILES])
            bqs = sb("bqs", [P, QTILES])
            bk = sb("bk", [P, QTILES])
            bv = sb("bv", [P, DI // P])
        stats = sb("stats", [P, TT, 6])
        mv = sb("mv", [P, TT, 2])
        vareps = sb("vareps", [P, TT])
        rstd = sb("rstd", [P, TT])
        h = sb("h", [P, TT, DM])
        hT = sb("hT", [P, DT, SEQ])
        QT = [sb(f"QT{n}", [P, QTILES, SEQ]) for n in range(2)]
        KT = [sb(f"KT{n}", [P, QTILES, SEQ]) for n in range(2)]
        V = [sb(f"V{n}", [P, TT, HEADS, dh + 1]) for n in range(2)]
        negmax = sb("negmax", [P, 4, TT])
        bias = sb("bias", [P, 4, TT]) if masked else negmax
        PR = [sb(f"PR{n}", [P, TT, SEQ]) for n in range(2)]
        PT = [sb(f"PT{n}", [P, TT, SEQ]) for n in range(2)]
        rsum = sb("rsum", [P, TT, G])
        AO = sb("AO", [P, TT, DI])
        AOT = sb("AOT", [P, DI // P, SEQ])
        if rope:
            cosx = sb("cosx", [P, 2, TT, dh])
            sinx = sb("sinx", [P, 2, TT, dh])
            RA = [sb(f"RA{n}", [P, BANK]) for n in range(2)]
            RB = [sb(f"RB{n}", [P, BANK]) for n in range(2)]
            QKR = [sb(f"QKR{n}", [P, TT, DI]) for n in range(2)]
        if masked:
            mask_u8 = sb("mask_u8", [P, TT, SEQ], U8)
            mask_f = sb("mask_f", [P, TT, SEQ])
            allmasked = sb("allmasked", [P, TT])
            anykey = sb("anykey", [P, TT])
        if masked or causal:
            maskneg = sb("maskneg", [P, TT, SEQ], BF16)
        if causal:
            maskneg_f = sb("maskneg_f", [P, TT, SEQ])

        SCO = [bank(f"SCO{n}") for n in range(2)]
        TRP = [bank(f"TRP{n}") for n in range(2)]
        O = [bank(f"O{n}") for n in range(TT)]
        FB = bank("FB")
        BB = bank("BB")

        s_load = sem("load")
        s_setup = sem("setup")
        s_ctx = [sem(f"ctx{n}") for n in range(2)]
        s_maskf = sem("maskf")
        s_stats = sem("stats")
        s_tick = sem("tick")
        s_mom = sem("moments")
        s_veps = sem("vareps")
        s_rstd = sem("rstd")
        s_h = sem("h")
        s_xb = sem("xb")
        s_ff = sem("front_filled")
        s_fa = sem("front_act")
        s_fd = sem("front_dve")
        s_rope = sem("rope")
        s_sc = sem("scores")
        s_nm = sem("negmax")
        s_mx = sem("bias") if masked else s_nm
        s_ex = sem("exp")
        s_tr = sem("transposed")
        s_pt = sem("ptcopied")
        s_av = sem("av")
        s_rs = sem("rsum")
        s_oe = sem("oevac")
        s_at = sem("aotrans")
        s_ba = sem("aoT")
        s_out = sem("outproj")
        s_x = sem("xdone")

        loads = [(wq[:, :, :], w["wq"].rearrange("(k p) n -> p k n", p=P)),
                 (wk[:, :, :], w["wk"].rearrange("(k p) n -> p k n", p=P)),
                 (wv[:, :, :], w["wv"].rearrange("(k p) n -> p k n", p=P)),
                 (wo[:, :, :], w["wo"].rearrange("(k p) n -> p k n", p=P)),
                 (bo[:, :], w["bo"].unsqueeze(0).broadcast_to([P, DM]))]
        if cross:
            loads += [(bq[:, :], w["bq"]), (bk[:, :], w["bk"]), (bv[:, :], w["bv"])]
        if rope:
            loads += [(cosx[:, :, :, :], w["cosx"]), (sinx[:, :, :, :], w["sinx"])]
        if masked:
            loads += [(mask_u8[:, :, :], w["mask"].rearrange("(t p) s -> p t s", p=P))]
        if causal:
            loads += [(maskneg_f[:, :, :], w["causal"])]
        LOADED = 16 * len(loads)
        SETUP = 2 + (1 if cross else 0) + (2 if masked else 0) + (1 if causal else 0)

        block = ctx.enter_context(nc.Block())

        @block.sync
        def _(sp):
            for dst, src in loads:
                sp.dma_start(dst, src).then_inc(s_load, 16)
            if cross:
                ctx_v = w["ctxT"].rearrange("(k p) n -> p k n", p=P)
                for b in range(2):
                    sp.dma_start(cT[b][:, :, :], ctx_v[:, :, b * SEQ:(b + 1) * SEQ]).then_inc(s_ctx[b], 16)
                with sp.Fori(1, BATCH // 2) as i:
                    for n in range(2):
                        sp.wait_ge(s_ff, i * (2 * NF) + NF * (n - 1))
                        sp.dma_start(cT[n][:, :, :], ctx_v[:, :, ds(i * (2 * SEQ) + n * SEQ, SEQ)])\
                          .then_inc(s_ctx[n], 16)

        @block.gpsimd
        def _(pool):
            def front(b):
                pool.wait_ge(s_mom, b * 2 + 2)
                pool.tensor_tensor(vareps[:, :], mv[:, :, 1], consts["ln_eps"][:, 0:TT], ALU.add).then_inc(s_veps, 1)
                pool.wait_ge(s_veps, b + 1)
                pool.tensor_tensor(rstd[:, :], vareps[:, :], consts["mhalf"][:, 0:TT], ALU.pow).then_inc(s_rstd, 1)
                pool.wait_ge(s_h, b * 2 + 2)
                for t in range(TT):
                    xt = x[:, ds(b * 2 + t, 1), :].rearrange("p a n -> p (a n)")
                    pool.tensor_tensor(xt, xt, bo[:, :], ALU.add).then_inc(s_xb, 1)

            def rotate(b):
                for which in range(2):
                    for n in range(4):
                        j = 1 + 4 * which + n
                        pool.wait_ge(s_fd, emptied(b, j)[1])
                        t, c = n // 2, n % 2
                        pool.tensor_tensor(QKR[which][:, t, c * BANK:(c + 1) * BANK], RA[n % 2][:, :],
                                           RB[n % 2][:, :], ALU.add).then_inc(s_rope, 1)

            def step(s, par, front_, heads, back):
                if front_:
                    front(s + 1)
                    if rope:
                        rotate(s + 1)

            pool.wait_ge(s_load, LOADED)
            front(0)
            if rope:
                rotate(0)
            seq_steps(pool, step)

        @block.vector
        def _(dve):
            dve.wait_ge(s_load, LOADED)
            n_setup = 0
            dve.sem_inc(s_x, 1)
            for n in range(2):
                dve.memset(V[n][:, :, :, dh:dh + 1], 1.0).then_inc(s_setup, 1)
                n_setup += 1
            if cross:
                dve.tensor_scalar(bqs[:, :], bq[:, :], SC, None, ALU.mult).then_inc(s_setup, 1)
                n_setup += 1
            if masked:
                dve.tensor_copy(mask_f[:, :, :], mask_u8[:, :, :]).then_inc(s_maskf, 1)
                dve.wait_ge(s_maskf, 1)
                dve.tensor_scalar(maskneg[:, :, :], mask_f[:, :, :], NEG, None, ALU.mult).then_inc(s_setup, 1)
                dve.tensor_reduce(allmasked[:, :], mask_f[:, :, :], AXX, ALU.min).then_inc(s_maskf, 1)
                dve.wait_ge(s_maskf, 2)
                dve.tensor_scalar(anykey[:, :], allmasked[:, :], -1.0, 1.0, ALU.mult, ALU.add).then_inc(s_setup, 1)
                n_setup += 2
            if causal:
                dve.tensor_copy(maskneg[:, :, :], maskneg_f[:, :, :]).then_inc(s_setup, 1)
                n_setup += 1
            assert n_setup == SETUP

            def front(k, b):
                if k == 0:
                    for t in range(TT):
                        dve.bn_stats(stats[:, t, :], x[:, ds(b * 2 + t, 1), :].rearrange("p a n -> p (a n)"))\
                           .then_inc(s_stats, 1)
                    dve.wait_ge(s_stats, b * 2 + 2)
                    dve.sem_inc(s_tick, 1)
                    for t in range(TT):
                        dve.bn_aggr(mv[:, t, :], stats[:, t, :]).then_inc(s_mom, 1)
                if k == 1:
                    dve.wait_ge(s_rstd, b + 1)
                    await_ge(dve, s_ff, (b - 1) * NF + 1)
                    for t in range(TT):
                        dve.tensor_scalar(h[:, t, :], x[:, ds(b * 2 + t, 1), :].rearrange("p a n -> p (a n)"),
                                          mv[:, t, 0:1], rstd[:, t:t + 1], ALU.subtract, ALU.mult).then_inc(s_h, 1)
                for j, (kind, n, e, slot) in enumerate(USES):
                    if e == "dve" and slot == k:
                        which = 0 if kind == "qr" else 1
                        t = n // 2
                        dve.wait_ge(s_ff, b * NF + j + 1)
                        await_ge(dve, s_rope, b * 8 + 4 * which + n - 1)
                        A = RA[n % 2][:, :].rearrange("p (h d) -> p h d", d=dh)
                        Bv = RB[n % 2][:, :].rearrange("p (h i two) -> p h i two", i=dh // 2, two=2)
                        q = FB[:, :].rearrange("p (h d) -> p h d", d=dh)
                        q2 = FB[:, :].rearrange("p (h i two) -> p h i two", i=dh // 2, two=2)
                        nh = BANK // dh
                        cos = cosx[:, which, t, :].unsqueeze(1).broadcast_to([P, nh, dh])
                        sn = [sinx[:, which, t, i * dh // 2:(i + 1) * dh // 2].unsqueeze(1).broadcast_to([P, nh, dh // 2])
                              for i in range(2)]
                        dve.tensor_tensor(A, q, cos, ALU.mult).then_inc(s_fd, 1)
                        dve.tensor_tensor(Bv[:, :, :, 0], q2[:, :, :, 1],
                                          sn[0], ALU.mult).then_inc(s_fd, 1)
                        dve.tensor_tensor(Bv[:, :, :, 1], q2[:, :, :, 0],
                                          sn[1], ALU.mult).then_inc(s_fd, 1)

            def o_evac(s, q):
                dve.wait_ge(s_av, s * HEADS + G * (q + 1))
                gq = s * NG + q
                for t in range(TT):
                    ov = O[t][:, 0:G * (dh + 1)].rearrange("p (g d) -> p g d", d=dh + 1)
                    dve.reciprocal(rsum[:, t, :], ov[:, :, dh]).then_inc(s_rs, 1)
                dve.wait_ge(s_rs, gq * 2 + 2)
                await_ge(dve, s_at, gq + 2 - NG)
                for t in range(TT):
                    ov = O[t][:, 0:G * (dh + 1)].rearrange("p (g d) -> p g d", d=dh + 1)
                    dve.tensor_tensor(AO[:, t, q * G * dh:(q + 1) * G * dh].rearrange("p (g d) -> p g d", d=dh),
                                      ov[:, :, 0:dh],
                                      rsum[:, t, :].unsqueeze(2).broadcast_to([P, G, dh]),
                                      ALU.mult).then_inc(s_oe, 1)

            def step(s, par, front_, heads, back):
                for k in range(HEADS if heads else 6):
                    g = s * HEADS + k
                    if front_:
                        front(k, s + 1)
                    if heads:
                        dve.wait_ge(s_sc, g + 1)
                        dve.reduce_max(negmax[:, k % 4, :], SCO[k % 2][:, :].rearrange("p (t s) -> p t s", t=TT),
                                       AXX, negate=True).then_inc(s_nm, 1)
                        if masked:
                            dve.wait_ge(s_nm, g + 1)
                            dve.tensor_tensor(bias[:, k % 4, :], negmax[:, k % 4, :], anykey[:, :], ALU.mult)\
                               .then_inc(s_mx, 1)
                    if (heads and k >= 1) or (k == 0 and back):
                        pk = (k - 1) % 2
                        dve.wait_ge(s_tr, g)
                        await_ge(dve, s_av, g - 2)
                        W = 3 * P if causal else TT * SEQ
                        dve.tensor_copy(PT[pk][:, :, :].rearrange("p a b -> p (a b)")[:, 0:W], TRP[pk][:, 0:W])\
                           .then_inc(s_pt, 1)
                    for q in range(NG):
                        slot = G * (q + 1) + 1
                        if slot < HEADS and heads and k == slot:
                            o_evac(s, q)
                        if slot >= HEADS and back and k == slot - HEADS:
                            o_evac(s - 1, q)
                    if back and k == 5:
                        dve.wait_ge(s_out, s + 1)
                        dve.wait_ge(s_xb, s * 2)
                        xs = x[:, ds(s * 2 - 2, 2), :].rearrange("p a n -> p (a n)")
                        dve.tensor_tensor(xs, BB[:, :], xs, ALU.add).then_inc(s_x, 1)

            for k in range(HEADS):
                front(k, 0)
            seq_steps(dve, step)
            dve.wait_ge(s_x, BATCH + 1)

        @block.scalar
        def _(act):
            act.wait_ge(s_load, LOADED)
            act.wait_ge(s_setup, SETUP)

            def front(k, b, par):
                for j, (kind, n, e, slot) in enumerate(USES):
                    if e != "act" or slot != k:
                        continue
                    act.wait_ge(s_ff, b * NF + j + 1)
                    if kind == "hT":
                        act.activation(hT[:, :, :].rearrange("p a b -> p (a b)"), FB[:, :], ACT.Copy).then_inc(s_fa, 1)
                    if kind in ("q", "k"):
                        for i in range(2):
                            dst = (QT if kind == "q" else KT)[par][:, 2 * n + i, :]
                            bcol = (bqs if kind == "q" else bk)[:, 2 * n + i:2 * n + i + 1]
                            act.activation(dst, FB[:, i * SEQ:(i + 1) * SEQ], ACT.Identity, bias=bcol,
                                           scale=SC if kind == "q" else 1.0).then_inc(s_fa, 1)
                    if kind in ("qT", "kT"):
                        dst = (QT if kind == "qT" else KT)[par][:, 2 * n:2 * n + 2, :]
                        act.activation(dst.rearrange("p a b -> p (a b)"), FB[:, :], ACT.Copy).then_inc(s_fa, 1)
                    if kind == "v":
                        if cross:
                            for_v = V[par][:, :, :, 0:dh]
                            src = FB[:, :].rearrange("p (t h d) -> p t h d", t=TT, d=dh)
                        else:
                            t, c = n // 2, n % 2
                            for_v = V[par][:, t, 8 * c:8 * c + 8, 0:dh]
                            src = FB[:, :].rearrange("p (h d) -> p h d", d=dh)
                        act.activation(for_v, src, ACT.Copy).then_inc(s_fa, 1)

            def aoT_copy(s, q):
                act.wait_ge(s_at, s * NG + q + 2)
                act.wait_ge(s_out, s + 1)
                for i in range(2):
                    src = BB[:, i * SEQ:(i + 1) * SEQ]
                    if cross:
                        act.activation(AOT[:, 2 * q + i, :], src, ACT.Identity, bias=bv[:, 2 * q + i:2 * q + i + 1])\
                           .then_inc(s_ba, 1)
                    else:
                        act.activation(AOT[:, 2 * q + i, :], src, ACT.Copy).then_inc(s_ba, 1)

            def step(s, par, front_, heads, back):
                for k in range(HEADS if heads else 6):
                    g = s * HEADS + k
                    if heads:
                        act.wait_ge(s_mx, g + 1)
                        await_ge(act, s_tr, g - 1)
                        for t in range(TT):
                            W = P * (t + 1) if causal else SEQ
                            act.activation(PR[k % 2][:, t, 0:W], SCO[k % 2][:, t * SEQ:t * SEQ + W], ACT.Exp,
                                           bias=bias[:, k % 4, t:t + 1],
                                           scale=anykey[:, t:t + 1] if masked else 1.0).then_inc(s_ex, 1)
                    if front_:
                        front(k, s + 1, 1 - par)
                    for q in range(NG):
                        slot = G * (q + 1) + 3
                        if slot < HEADS and heads and k == slot:
                            aoT_copy(s, q)
                        if slot >= HEADS and back and k == slot - HEADS:
                            aoT_copy(s - 1, q)

            for k in range(HEADS):
                front(k, 0, 0)
            seq_steps(act, step)

        @block.tensor
        def _(pe):
            pe.wait_ge(s_load, LOADED)
            pe.wait_ge(s_setup, SETUP)
            pe.sem_inc(s_at, 1)
            pe.sem_inc(s_out, 1)

            def front(k, b, par):
                for j, (kind, n, _, slot) in enumerate(USES):
                    if slot != k:
                        continue
                    if j == 0:
                        e, v = emptied(b - 1, NF - 1)
                        pe.wait_ge(s_h, b * 2 + 2)
                    else:
                        e, v = emptied(b, j - 1)
                    await_ge(pe, s_fa if e == "act" else s_fd, v)
                    if kind == "hT":
                        for d in range(DT):
                            for t in range(TT):
                                c = d * SEQ + t * P
                                last = pe.transpose(FB[:, c:c + P], h[:, t, d * P:(d + 1) * P], ident[:, :])
                    if cross and kind in ("k", "v"):
                        pe.wait_ge(s_ctx[par], b * 8 + 16 - 8 * par)
                    if kind in ("q", "k"):
                        wt = wq if kind == "q" else wk
                        for i in range(2):
                            m = 2 * n + i
                            for kk in range(DT):
                                rhs = hT[:, kk, :] if kind == "q" else cT[par][:, kk, :]
                                last = pe.matmul(FB[:, i * SEQ:(i + 1) * SEQ], wt[:, kk, m * P:(m + 1) * P], rhs,
                                                 start=(kk == 0), stop=(kk == DT - 1))
                    if kind in ("qr", "kr", "v") and not cross:
                        wt = {"qr": wq, "kr": wk, "v": wv}[kind]
                        t, c = n // 2, n % 2
                        for kk in range(DT):
                            last = pe.matmul(FB[:, :], hT[:, kk, t * P:(t + 1) * P], wt[:, kk, c * BANK:(c + 1) * BANK],
                                             start=(kk == 0), stop=(kk == DT - 1))
                    if kind == "v" and cross:
                        for t in range(TT):
                            for kk in range(DT):
                                last = pe.matmul(FB[:, t * DI:(t + 1) * DI], cT[par][:, kk, t * P:(t + 1) * P],
                                                 wv[:, kk, :], start=(kk == 0), stop=(kk == DT - 1))
                    if kind in ("qT", "kT"):
                        which = 0 if kind == "qT" else 1
                        pe.wait_ge(s_rope, b * 8 + 4 * (which + 1))
                        for i in range(2):
                            for t in range(TT):
                                m = 2 * n + i
                                last = pe.transpose(FB[:, i * SEQ + t * P:i * SEQ + (t + 1) * P],
                                                    QKR[which][:, t, m * P:(m + 1) * P], ident[:, :])
                    last.then_inc(s_ff, 1)

            def scores(s, k, par):
                g = s * HEADS + k
                if k == 0:
                    pe.wait_ge(s_fa, emptied(s, NF - 1)[1])
                await_ge(pe, s_ex, g * 2 - 2)
                bank_ = SCO[k % 2]
                tile, r = k // HPT, PITCH * (k % HPT)
                add_mask = masked or causal
                for t in range(TT):
                    W = P * (t + 1) if causal else SEQ
                    last = pe.matmul(bank_[:, t * SEQ:t * SEQ + W], QT[par][r:r + dh, tile, t * P:(t + 1) * P],
                                     KT[par][r:r + dh, tile, 0:W], start=(t == 0 or not add_mask),
                                     stop=not add_mask, skip_group_check=add_mask)
                if add_mask:
                    last = pe.matmul(bank_[:, :], ident_bf[:, :], maskneg[:, :, :].rearrange("p t s -> p (t s)"),
                                     start=False, stop=True, skip_group_check=True)
                last.then_inc(s_sc, 1)

            def transposes(g, k):
                pe.wait_ge(s_ex, g * 2 + 2)
                await_ge(pe, s_pt, g - 1)
                for st in range(TT):
                    for t in range(TT):
                        if causal and st > t:
                            continue
                        c = st * SEQ + t * P if not causal else (2 * P if st else t * P)
                        last = pe.transpose(TRP[k % 2][:, c:c + P], PR[k % 2][:, t, st * P:(st + 1) * P], ident[:, :])
                last.then_inc(s_tr, 1)

            def av(s, g, k, par):
                pe.wait_ge(s_pt, g + 1)
                if k % G == 0:
                    await_ge(pe, s_oe, (s * NG + k // G) * 2)
                for t in range(TT):
                    n_st = t + 1 if causal else TT
                    for st in range(n_st):
                        c = st * SEQ + t * P if not causal else (2 * P if st else t * P)
                        o = (k % G) * (dh + 1)
                        last = pe.matmul(O[t][:, o:o + dh + 1], PT[k % 2][:, :, :].rearrange("p a b -> p (a b)")[:, c:c + P],
                                         V[par][:, st, k, :], start=(st == 0), stop=(st == n_st - 1))
                last.then_inc(s_av, 1)

            def ao_transposes(s, q):
                pe.wait_ge(s_oe, (s * NG + q + 1) * 2)
                if q == 0:
                    pe.wait_ge(s_x, s + 1)
                else:
                    pe.wait_ge(s_ba, (s * NG + q) * 2)
                for i in range(2):
                    for t in range(TT):
                        last = pe.transpose(BB[:, i * SEQ + t * P:i * SEQ + (t + 1) * P],
                                            AO[:, t, (2 * q + i) * P:(2 * q + i + 1) * P], ident[:, :])
                last.then_inc(s_at, 1)

            def step(s, par, front_, heads, back):
                for k in range(HEADS if heads else 6):
                    g = s * HEADS + k
                    if heads:
                        scores(s, k, par)
                    if (heads and k >= 1) or (k == 0 and back):
                        transposes(g - 1, (k - 1) % HEADS)
                    if heads and k >= 2:
                        av(s, g - 2, k - 2, par)
                    if k < 2 and back:
                        av(s - 1, g - 2, k + HEADS - 2, 1 - par)
                    if front_:
                        front(k, s + 1, 1 - par)
                    for q in range(NG):
                        slot = G * (q + 1) + 3
                        if slot < HEADS and heads and k == slot:
                            ao_transposes(s, q)
                        if slot >= HEADS and back and k == slot - HEADS:
                            ao_transposes(s - 1, q)
                    if back and k == 5:
                        pe.wait_ge(s_ba, s * NG * 2)
                        for t in range(TT):
                            for kk in range(DI // P):
                                last = pe.matmul(BB[:, t * DM:(t + 1) * DM], AOT[:, kk, t * P:(t + 1) * P], wo[:, kk, :],
                                                 start=(kk == 0), stop=(kk == DI // P - 1))
                        last.then_inc(s_out, 1)

            for k in range(HEADS):
                front(k, 0, 0)
            seq_steps(pe, step)


def retention_layer(nc, name, x, consts, w):
    dh = 16
    QTILES, HPT, PITCH = 4, 4, 32
    PTW = 3 * P
    RING = 4
    ident = consts["ident"]
    USES = [("hT", 0, "act", 1), ("q", 0, "dve", 2), ("q", 1, "dve", 3), ("k", 0, "dve", 4), ("k", 1, "dve", 5),
            ("v", 0, "act", 6), ("g", 0, "dve", 7)]
    NF = len(USES)
    BACK_STEPS = 11

    def emptied(b, j):
        e = USES[j][2]
        return e, b * sum(u[2] == e for u in USES) + sum(u[2] == e for u in USES[:j + 1])

    with ExitStack() as ctx:
        sc = Scope(nc, ctx, name)
        sb, bank, sem = sc.sb, sc.bank, sc.sem
        wq = sb("wq", [P, DT, QTILES * P])
        wk = sb("wk", [P, DT, QTILES * P])
        wv = sb("wv", [P, DT, DM])
        wg = sb("wg", [P, DT, DM])
        wo = sb("wo", [P, DT, DM])
        bo = sb("bo", [P, DM])
        bg = sb("bg", [P, DM])
        lng = sb("lng", [P, DM])
        lnb = sb("lnb", [P, DM])
        qdec = sb("qdec", [P, QTILES, SEQ])
        kdec = sb("kdec", [P, QTILES, SEQ])
        keep = sb("keep", [P, PTW])
        stats = sb("stats", [P, TT, 6])
        mv = sb("mv", [P, TT, 2])
        vareps = sb("vareps", [P, TT])
        rstd = sb("rstd", [P, TT])
        h = sb("h", [P, TT, DM])
        hT = sb("hT", [P, DT, SEQ])
        QT = [sb(f"QT{n}", [P, QTILES, SEQ]) for n in range(2)]
        KT = [sb(f"KT{n}", [P, QTILES, SEQ]) for n in range(2)]
        V = [sb(f"V{n}", [P, TT, HEADS, dh]) for n in range(2)]
        gate = sb("gate", [P, TT, DM])
        th = sb("th", [P, TT, DM])
        swish2 = [sb(f"swish2_{n}", [P, TT, DM]) for n in range(2)]
        PT = [sb(f"PT{n}", [P, PTW]) for n in range(RING)]
        R = sb("R", [P, TT, DM])
        stats2 = sb("stats2", [P, TT, 6])
        mv2 = sb("mv2", [P, TT, 2])
        vareps2 = sb("vareps2", [P, TT])
        rstd2 = sb("rstd2", [P, TT])
        Y = sb("Y", [P, TT, DM])
        YT = sb("YT", [P, DT, SEQ])

        SCO = [bank(f"SCO{n}") for n in range(RING)]
        O = [bank(f"O{n}") for n in range(TT)]
        FB = bank("FB")
        BB = bank("BB")

        s_load = sem("load")
        s_xload = sem("xload")
        s_stats = sem("stats")
        s_tick = sem("tick")
        s_mom = sem("moments")
        s_veps = sem("vareps")
        s_rstd = sem("rstd")
        s_h = sem("h")
        s_xb = sem("xb")
        s_ff = sem("front_filled")
        s_fa = sem("front_act")
        s_fd = sem("front_dve")
        s_th = sem("tanh")
        s_sw = sem("swish")
        s_sc = sem("scores")
        s_pt = sem("pt")
        s_av = sem("av")
        s_oe = sem("oevac")
        s_st2 = sem("stats2")
        s_mom2 = sem("moments2")
        s_veps2 = sem("vareps2")
        s_rstd2 = sem("rstd2")
        s_y1 = sem("y_normed")
        s_y2 = sem("y_scaled")
        s_y3 = sem("y_shifted")
        s_y4 = sem("y_gated")
        s_yt = sem("y_transposed")
        s_ya = sem("yT")
        s_out = sem("outproj")
        s_x = sem("xdone")

        loads = [(t[:, :, :], w[n].rearrange("(k p) n -> p k n", p=P))
                 for t, n in ((wq, "wq"), (wk, "wk"), (wv, "wv"), (wg, "wg"), (wo, "wo"))]
        loads += [(t[:, :], w[n].unsqueeze(0).broadcast_to([P, DM]))
                  for t, n in ((bo, "bo"), (bg, "bg"), (lng, "gamma"), (lnb, "beta"))]
        loads += [(qdec[:, :, :], w["qdec"]), (kdec[:, :, :], w["kdec"]), (keep[:, :], w["keep"])]
        loads += [(consts["ident"][:, :], w["ident"]), (consts["mhalf"][:, :], w["mhalf"]),
                  (consts["ln_eps"][:, :], w["ln_eps"]), (consts["ret_eps"][:, :], w["ret_eps"])]
        LOADED = 16 * len(loads)
        x_v = w["x"].rearrange("b (t p) n -> p (b t) n", p=P)

        block = ctx.enter_context(nc.Block())

        @block.sync
        def _(sp):
            sp.dma_start(x[:, :, :], x_v).then_inc(s_xload, 16)
            for dst, src in loads:
                sp.dma_start(dst, src).then_inc(s_load, 16)

        @block.gpsimd
        def _(pool):
            pool.wait_ge(s_load, LOADED)

            def front(b):
                pool.wait_ge(s_mom, b * 2 + 2)
                pool.tensor_tensor(vareps[:, :], mv[:, :, 1], consts["ln_eps"][:, 0:TT], ALU.add).then_inc(s_veps, 1)
                pool.wait_ge(s_veps, b + 1)
                pool.tensor_tensor(rstd[:, :], vareps[:, :], consts["mhalf"][:, 0:TT], ALU.pow).then_inc(s_rstd, 1)
                pool.wait_ge(s_h, b * 2 + 2)
                for t in range(TT):
                    xt = x[:, ds(b * 2 + t, 1), :].rearrange("p a n -> p (a n)")
                    pool.tensor_tensor(xt, xt, bo[:, :], ALU.add).then_inc(s_xb, 1)

            def back_norm(b):
                pool.wait_ge(s_mom2, b * 2 + 2)
                pool.tensor_tensor(vareps2[:, :], mv2[:, :, 1], consts["ret_eps"][:, 0:TT], ALU.add).then_inc(s_veps2, 1)
                pool.wait_ge(s_veps2, b + 1)
                pool.tensor_tensor(rstd2[:, :], vareps2[:, :], consts["mhalf"][:, 0:TT], ALU.pow).then_inc(s_rstd2, 1)

            def back_affine(b):
                for t in range(TT):
                    pool.wait_ge(s_y1, b * 2 + t + 2)
                    pool.tensor_tensor(Y[:, t, :], Y[:, t, :], lng[:, :], ALU.mult).then_inc(s_y2, 1)
                for t in range(TT):
                    pool.wait_ge(s_y2, b * 2 + t + 1)
                    pool.tensor_tensor(Y[:, t, :], Y[:, t, :], lnb[:, :], ALU.add).then_inc(s_y3, 1)

            def step(s, par, front_, heads, back):
                if front_:
                    front(s + 1)
                if back:
                    back_norm(s - 1)
                    back_affine(s - 1)

            front(0)
            seq_steps(pool, step)

        @block.vector
        def _(dve):
            dve.sem_inc(s_x, 1)
            dve.sem_inc(s_y1, 1)
            dve.wait_ge(s_xload, 16)
            dve.wait_ge(s_load, LOADED)

            def front(k, b, par):
                if k == 0:
                    for t in range(TT):
                        dve.bn_stats(stats[:, t, :], x[:, ds(b * 2 + t, 1), :].rearrange("p a n -> p (a n)"))\
                           .then_inc(s_stats, 1)
                    dve.wait_ge(s_stats, b * 2 + 2)
                    dve.sem_inc(s_tick, 1)
                    for t in range(TT):
                        dve.bn_aggr(mv[:, t, :], stats[:, t, :]).then_inc(s_mom, 1)
                if k == 1:
                    dve.wait_ge(s_rstd, b + 1)
                    await_ge(dve, s_ff, (b - 1) * NF + 1)
                    for t in range(TT):
                        dve.tensor_scalar(h[:, t, :], x[:, ds(b * 2 + t, 1), :].rearrange("p a n -> p (a n)"),
                                          mv[:, t, 0:1], rstd[:, t:t + 1], ALU.subtract, ALU.mult).then_inc(s_h, 1)
                for j, (kind, n, e, slot) in enumerate(USES):
                    if slot != k or e != "dve":
                        continue
                    dve.wait_ge(s_ff, b * NF + j + 1)
                    if kind in ("q", "k"):
                        dst = (QT if kind == "q" else KT)[par][:, 2 * n:2 * n + 2, :]
                        dec = (qdec if kind == "q" else kdec)[:, 2 * n:2 * n + 2, :]
                        dve.tensor_tensor(dst.rearrange("p a b -> p (a b)"), FB[:, :], dec.rearrange("p a b -> p (a b)"),
                                          ALU.mult).then_inc(s_fd, 1)
                    if kind == "g":
                        dve.tensor_tensor(gate[:, :, :], FB[:, :].rearrange("p (t n) -> p t n", t=TT),
                                          bg[:, :].unsqueeze(1).broadcast_to([P, TT, DM]), ALU.add).then_inc(s_fd, 1)
                if k == 9:
                    dve.wait_ge(s_th, b + 1)
                    dve.scalar_tensor_tensor(swish2[par][:, :, :], th[:, :, :], 1.0, gate[:, :, :], ALU.add, ALU.mult)\
                       .then_inc(s_sw, 1)

            def back_part(k, b, par):
                if k == 1:
                    for t in range(TT):
                        dve.wait_ge(s_oe, b * 2 + t + 1)
                        dve.bn_stats(stats2[:, t, :], R[:, t, :]).then_inc(s_st2, 1)
                    dve.wait_ge(s_st2, b * 2 + 2)
                    dve.sem_inc(s_tick, 1)
                    for t in range(TT):
                        dve.bn_aggr(mv2[:, t, :], stats2[:, t, :]).then_inc(s_mom2, 1)
                if k == 3:
                    dve.wait_ge(s_rstd2, b + 1)
                    for t in range(TT):
                        dve.tensor_scalar(Y[:, t, :], R[:, t, :], mv2[:, t, 0:1], rstd2[:, t:t + 1],
                                          ALU.subtract, ALU.mult).then_inc(s_y1, 1)
                if k == 6:
                    dve.wait_ge(s_sw, b + 1)
                    for t in range(TT):
                        dve.wait_ge(s_y3, b * 2 + t + 1)
                        dve.scalar_tensor_tensor(Y[:, t, :], Y[:, t, :], 0.5, swish2[par][:, t, :], ALU.mult, ALU.mult)\
                           .then_inc(s_y4, 1)
                if k == 9:
                    dve.wait_ge(s_out, b + 2)
                    dve.wait_ge(s_xb, b * 2 + 2)
                    xs = x[:, ds(b * 2, 2), :].rearrange("p a n -> p (a n)")
                    dve.tensor_tensor(xs, BB[:, :], xs, ALU.add).then_inc(s_x, 1)

            def step(s, par, front_, heads, back):
                for k in range(HEADS if heads else BACK_STEPS):
                    g = s * HEADS + k
                    if front_:
                        front(k, s + 1, 1 - par)
                    if heads:
                        dve.wait_ge(s_sc, g + 1)
                        await_ge(dve, s_av, g - RING + 1)
                        dve.tensor_tensor(PT[k % RING][:, :], SCO[k % RING][:, 0:PTW], keep[:, :], ALU.mult)\
                           .then_inc(s_pt, 1)
                    if back:
                        back_part(k, s - 1, 1 - par)

            for k in range(HEADS):
                front(k, 0, 0)
            seq_steps(dve, step)
            dve.wait_ge(s_x, BATCH + 1)

        @block.scalar
        def _(act):
            def front(k, b, par):
                for j, (kind, n, e, slot) in enumerate(USES):
                    if e != "act" or slot != k:
                        continue
                    act.wait_ge(s_ff, b * NF + j + 1)
                    dst = hT[:, :, :] if kind == "hT" else V[par][:, :, :, :].rearrange("p t h d -> p t (h d)")
                    act.activation(dst.rearrange("p a b -> p (a b)"), FB[:, :], ACT.Copy).then_inc(s_fa, 1)
                if k == 8:
                    act.wait_ge(s_fd, emptied(b, NF - 1)[1])
                    await_ge(act, s_sw, b)
                    act.activation(th[:, :, :], gate[:, :, :], ACT.Tanh, scale=0.5).then_inc(s_th, 1)

            def back_part(k, b):
                if k == 0:
                    act.wait_ge(s_av, b * HEADS + HEADS)
                    act.wait_ge(s_y1, b * 2 + 1)
                    for t in range(TT):
                        act.activation(R[:, t, :], O[t][:, 0:DM], ACT.Copy).then_inc(s_oe, 1)
                if k == 7:
                    act.wait_ge(s_yt, b + 1)
                    act.wait_ge(s_out, b + 1)
                    act.activation(YT[:, :, :].rearrange("p a b -> p (a b)"), BB[:, :], ACT.Copy).then_inc(s_ya, 1)

            def step(s, par, front_, heads, back):
                for k in range(HEADS if heads else BACK_STEPS):
                    if back:
                        back_part(k, s - 1)
                    if front_:
                        front(k, s + 1, 1 - par)

            for k in range(HEADS):
                front(k, 0, 0)
            seq_steps(act, step)

        @block.tensor
        def _(pe):
            pe.sem_inc(s_out, 1)
            pe.wait_ge(s_load, LOADED)

            def front(k, b, par):
                for j, (kind, n, _, slot) in enumerate(USES):
                    if slot != k:
                        continue
                    if j == 0:
                        e, v = emptied(b - 1, NF - 1)
                        pe.wait_ge(s_h, b * 2 + 2)
                    else:
                        e, v = emptied(b, j - 1)
                    await_ge(pe, s_fa if e == "act" else s_fd, v)
                    if kind == "hT":
                        for d in range(DT):
                            for t in range(TT):
                                c = d * SEQ + t * P
                                last = pe.transpose(FB[:, c:c + P], h[:, t, d * P:(d + 1) * P], ident[:, :])
                    if kind in ("q", "k"):
                        wt = wq if kind == "q" else wk
                        for i in range(2):
                            m = 2 * n + i
                            for kk in range(DT):
                                last = pe.matmul(FB[:, i * SEQ:(i + 1) * SEQ], wt[:, kk, m * P:(m + 1) * P],
                                                 hT[:, kk, :], start=(kk == 0), stop=(kk == DT - 1))
                    if kind in ("v", "g"):
                        wt = wv if kind == "v" else wg
                        for t in range(TT):
                            for kk in range(DT):
                                last = pe.matmul(FB[:, t * DM:(t + 1) * DM], hT[:, kk, t * P:(t + 1) * P],
                                                 wt[:, kk, :], start=(kk == 0), stop=(kk == DT - 1))
                    last.then_inc(s_ff, 1)

            def scores(s, k, par):
                g = s * HEADS + k
                if k == 0:
                    pe.wait_ge(s_fa, emptied(s, 5)[1])
                    pe.wait_ge(s_fd, emptied(s, 4)[1])
                await_ge(pe, s_pt, g - RING + 1)
                tile, r = k // HPT, PITCH * (k % HPT)
                pe.matmul(SCO[k % RING][:, 0:SEQ], KT[par][r:r + dh, tile, 0:P], QT[par][r:r + dh, tile, :],
                          start=True, stop=True)
                pe.matmul(SCO[k % RING][:, SEQ:PTW], KT[par][r:r + dh, tile, P:SEQ], QT[par][r:r + dh, tile, P:SEQ],
                          start=True, stop=True).then_inc(s_sc, 1)

            def av(s, g, k, par):
                pe.wait_ge(s_pt, g + 1)
                if k == 0:
                    await_ge(pe, s_oe, s * 2)
                for t in range(TT):
                    for st in range(t + 1):
                        c = 2 * P if st else t * P
                        last = pe.matmul(O[t][:, k * dh:(k + 1) * dh], PT[k % RING][:, c:c + P], V[par][:, st, k, :],
                                         start=(st == 0), stop=(st == t))
                last.then_inc(s_av, 1)

            def back_part(k, b):
                if k == 7:
                    pe.wait_ge(s_y4, b * 2 + 2)
                    pe.wait_ge(s_x, b + 1)
                    for d in range(DT):
                        for t in range(TT):
                            c = d * SEQ + t * P
                            last = pe.transpose(BB[:, c:c + P], Y[:, t, d * P:(d + 1) * P], ident[:, :])
                    last.then_inc(s_yt, 1)
                if k == 9:
                    pe.wait_ge(s_ya, b + 1)
                    for t in range(TT):
                        for kk in range(DT):
                            last = pe.matmul(BB[:, t * DM:(t + 1) * DM], YT[:, kk, t * P:(t + 1) * P], wo[:, kk, :],
                                             start=(kk == 0), stop=(kk == DT - 1))
                    last.then_inc(s_out, 1)

            def step(s, par, front_, heads, back):
                for k in range(HEADS if heads else BACK_STEPS):
                    g = s * HEADS + k
                    if heads:
                        scores(s, k, par)
                    if heads and k >= 1:
                        av(s, g - 1, k - 1, par)
                    if k == 0 and back:
                        av(s - 1, g - 1, HEADS - 1, 1 - par)
                    if front_:
                        front(k, s + 1, 1 - par)
                    if back:
                        back_part(k, s - 1)

            for k in range(HEADS):
                front(k, 0, 0)
            seq_steps(pe, step)


def expert_layer(nc, name, x, consts, w, top, hidden):
    E = 8
    ROWS = BATCH * SEQ
    GR = SEQ
    GROUPS = top * ROWS // GR + E
    SLOTS = GROUPS * GR
    MOST = ROWS // GR
    glu_bias = "b1" in w
    MT = [(m * P, min(P, hidden - m * P)) for m in range((hidden + P - 1) // P)]
    NM = len(MT)
    WHOLE = hidden // P
    REST = hidden - WHOLE * P
    ident = consts["ident"]
    xs_rows = nc.dram_tensor(f"{name}_sorted", (SLOTS, DM), F32).ap()
    ys_rows = nc.dram_tensor(f"{name}_outputs", (SLOTS, DM), F32).ap()

    with ExitStack() as outer:
        keep_ = Scope(nc, outer, name)
        slot_u = keep_.sb("slot_u", [P, top, TILES], U32)
        expert_i = keep_.sb("expert_i", [P, GROUPS], I32)
        weight = keep_.sb("weight", [P, top, TILES])
        route_rows(nc, name, x, consts, w, top, E, GR, GROUPS, MOST, xs_rows, slot_u, expert_i, weight)

        with ExitStack() as ctx:
            sc = Scope(nc, ctx, name + "m")
            sb, bank, sem = sc.sb, sc.bank, sc.sem
            WA = [sb(f"WA{n}", [P, DT, hidden]) for n in range(2)]
            WG = [sb(f"WG{n}", [P, DT, hidden]) for n in range(2)]
            WD = [sb(f"WD{n}", [P, NM, DM]) for n in range(2)]
            if glu_bias:
                B1 = [sb(f"B1{n}", [P, 2 * NM]) for n in range(2)]
                B2 = [sb(f"B2{n}", [P, DM]) for n in range(2)]
            XR = [sb(f"XR{n}", [P, TT, DM]) for n in range(2)]
            XT = [sb(f"XT{n}", [P, DT, SEQ]) for n in range(2)]
            SG = [sb(f"SG{n}", [P, SEQ]) for n in range(4)]
            HT = [sb(f"HT{n}", [P, SEQ]) for n in range(4)]
            YS = [sb(f"YS{n}", [P, TT, DM]) for n in range(2)]
            U = [bank(f"U{n}") for n in range(4)]
            Y = [bank(f"Y{n}") for n in range(TT)]
            XB = bank("XB")
            s_w = [sem(f"weights{n}") for n in range(2)]
            s_xt = sem("x_transposed")
            s_xc = sem("xT")
            s_up = sem("up")
            s_sg = sem("sigmoid")
            s_ht = sem("hidden")
            s_dn = sem("down")
            s_ye = sem("y_out")
            s_ys = [sem(f"y_stored{n}") for n in range(2)]
            s_tick = sem("tick")
            W_DMAS = 4 + (1 if REST else 0) + (2 if glu_bias else 0)

            def pairs(eng, body):
                with eng.Fori(1, GROUPS // 2) as i:
                    for n in range(2):
                        body(i * 2 + n, n)

            block = ctx.enter_context(nc.Block())

            @block.sync
            def _(sp):
                def load(g, n):
                    e = sp.value_load(expert_i[0:1, ds(g, 1)], min_val=0, max_val=E - 1)
                    if not (isinstance(g, int) and g < 2):
                        sp.wait_ge(s_dn, g * NM - NM)
                        if glu_bias:
                            sp.wait_ge(s_ye, g * 2 - 2)
                    if glu_bias:
                        w1 = w["w1"][ds(e, 1)].rearrange("a (k p) n -> p (a k) n", p=P)
                        parts = [(WA[n][:, :, :], w1[:, :, 0:hidden]), (WG[n][:, :, :], w1[:, :, hidden:2 * hidden]),
                                 (B1[n][:, :], w["b1"][ds(e, 1)].rearrange("a p m -> p (a m)")),
                                 (B2[n][:, :], w["b2"][ds(e, 1), :].broadcast_to([P, DM]))]
                    else:
                        parts = [(WA[n][:, :, :], w["up"][ds(e, 1)].rearrange("a (k p) n -> p (a k) n", p=P)),
                                 (WG[n][:, :, :], w["gate"][ds(e, 1)].rearrange("a (k p) n -> p (a k) n", p=P))]
                    wd = w["w2" if glu_bias else "down"][ds(e, 1)].rearrange("a f n -> (a f) n")
                    parts += [(WD[n][:, 0:WHOLE, :], wd[0:WHOLE * P, :].rearrange("(m p) n -> p m n", p=P))]
                    if REST:
                        parts += [(WD[n][0:REST, WHOLE, :], wd[WHOLE * P:hidden, :])]
                    parts += [(XR[n][:, :, :], xs_rows[ds(g * GR, GR), :].rearrange("(t p) n -> p t n", p=P))]
                    assert len(parts) == W_DMAS
                    for dst, src in parts:
                        sp.dma_start(dst, src).then_inc(s_w[n], 16)
                load(0, 0)
                load(1, 1)
                pairs(sp, load)

            @block.gpsimd
            def _(pool):
                def store(g, n):
                    pool.wait_ge(s_ye, g * 2 + 2)
                    pool.sem_inc(s_tick, 1)
                    pool.dma_start(ys_rows[ds(g * GR, GR), :].rearrange("(t p) n -> p t n", p=P), YS[n][:, :, :])\
                        .then_inc(s_ys[n], 16)
                store(0, 0)
                store(1, 1)
                pairs(pool, store)
                for n in range(2):
                    pool.wait_ge(s_ys[n], 16 * (GROUPS // 2))

            def arrived(g, n):
                return g * (8 * W_DMAS) + 8 * W_DMAS * (2 - n)

            @block.tensor
            def _(pe):
                def x_transposes(g, n):
                    pe.wait_ge(s_w[n], arrived(g, n))
                    await_ge(pe, s_xc, g)
                    for d in range(DT):
                        for t in range(TT):
                            c = d * SEQ + t * P
                            last = pe.transpose(XB[:, c:c + P], XR[n][:, t, d * P:(d + 1) * P], ident[:, :])
                    last.then_inc(s_xt, 1)

                def up(g, n, m):
                    c, size = MT[m]
                    if m == 0:
                        pe.wait_ge(s_xc, g + 1)
                    await_ge(pe, s_ht, g * NM + (m - 3))
                    u = U[m % 4] if NM % 4 == 0 else U[(m + (NM % 4) * n) % 4]
                    for half, wt in enumerate((WA, WG)):
                        for kk in range(DT):
                            last = pe.matmul(u[0:size, half * SEQ:(half + 1) * SEQ], wt[n][:, kk, c:c + size],
                                             XT[n][:, kk, :], start=(kk == 0), stop=(kk == DT - 1))
                    last.then_inc(s_up, 1)

                def down(g, n, m):
                    size = MT[m][1]
                    pe.wait_ge(s_ht, g * NM + m + 1)
                    if m == 0:
                        await_ge(pe, s_ye, g * 2)
                    for t in range(TT):
                        last = pe.matmul(Y[t][:, 0:DM], HT[m % 4 if NM % 4 == 0 else (m + (NM % 4) * n) % 4][0:size, t * P:(t + 1) * P],
                                         WD[n][0:size, m, :], start=(m == 0), stop=(m == NM - 1))
                    last.then_inc(s_dn, 1)

                def group(g, n, ahead=True):
                    for m in range(NM):
                        up(g, n, m)
                        if m >= 2:
                            down(g, n, m - 2)
                        if m == 4 and ahead:
                            x_transposes(g + 1, 1 - n)
                    down(g, n, NM - 2)
                    down(g, n, NM - 1)

                x_transposes(0, 0)
                group(0, 0)
                group(1, 1)
                with pe.Fori(1, GROUPS // 2 - 1) as i:
                    for n in range(2):
                        group(i * 2 + n, n)
                group(GROUPS - 2, 0)
                group(GROUPS - 1, 1, ahead=False)

            def ring(n, m):
                return m % 4 if NM % 4 == 0 else (m + (NM % 4) * n) % 4

            @block.scalar
            def _(act):
                def x_copy(g, n):
                    act.wait_ge(s_xt, g + 1)
                    act.activation(XT[n][:, :, :].rearrange("p a b -> p (a b)"), XB[:, :], ACT.Copy).then_inc(s_xc, 1)

                def group(g, n, ahead=True):
                    for m in range(NM):
                        size = MT[m][1]
                        act.wait_ge(s_up, g * NM + m + 1)
                        bias = B1[n][0:size, NM + m:NM + m + 1] if glu_bias else 0.0
                        act.activation(SG[ring(n, m)][0:size, :], U[ring(n, m)][0:size, SEQ:2 * SEQ],
                                       ACT.Sigmoid if glu_bias else ACT.Silu, bias=bias).then_inc(s_sg, 1)
                        if m == 4 and ahead:
                            x_copy(g + 1, 1 - n)

                x_copy(0, 0)
                group(0, 0)
                group(1, 1)
                with act.Fori(1, GROUPS // 2 - 1) as i:
                    for n in range(2):
                        group(i * 2 + n, n)
                group(GROUPS - 2, 0)
                group(GROUPS - 1, 1, ahead=False)

            @block.vector
            def _(dve):
                def group(g, n):
                    for m in range(NM):
                        size = MT[m][1]
                        r = ring(n, m)
                        dve.wait_ge(s_sg, g * NM + m + 1)
                        await_ge(dve, s_dn, g * NM + (m - 3))
                        a = U[r][0:size, 0:SEQ]
                        if glu_bias:
                            dve.scalar_tensor_tensor(HT[r][0:size, :], a, B1[n][0:size, m:m + 1], SG[r][0:size, :],
                                                     ALU.add, ALU.mult).then_inc(s_ht, 1)
                        else:
                            dve.tensor_tensor(HT[r][0:size, :], a, SG[r][0:size, :], ALU.mult).then_inc(s_ht, 1)
                    dve.wait_ge(s_dn, g * NM + NM)
                    if not (isinstance(g, int) and g < 2):
                        dve.wait_ge(s_ys[n], g * 8 - 8 * n)
                    for t in range(TT):
                        if glu_bias:
                            dve.tensor_tensor(YS[n][:, t, :], Y[t][:, 0:DM], B2[n][:, :], ALU.add).then_inc(s_ye, 1)
                        else:
                            dve.tensor_copy(YS[n][:, t, :], Y[t][:, 0:DM]).then_inc(s_ye, 1)

                group(0, 0)
                group(1, 1)
                pairs(dve, group)

        combine_rows(nc, name, x, top, ys_rows, slot_u, weight)


def route_rows(nc, name, x, consts, w, top, E, GR, GROUPS, MOST, xs_rows, slot_u, expert_i, weight):
    ZW = 2048
    SLOTS = GROUPS * GR
    ZDMAS = SLOTS * DM // (P * ZW)
    ident = consts["ident"]
    with ExitStack() as ctx:
        sc = Scope(nc, ctx, name + "r")
        sb, bank, sem = sc.sb, sc.bank, sc.sem
        zeros = sb("zeros", [P, ZW])
        router = sb("router", [P, DT, E])
        if "router_b" in w:
            rbias = sb("rbias", [P, E])
        prefix_f = sb("prefix_f", [P, P])
        prefix = sb("prefix", [P, P], BF16)
        ones = sb("ones", [P, P], BF16)
        iota = sb("iota", [P, 32])
        stats = sb("stats", [P, TILES, 6])
        mv = sb("mv", [P, TILES, 2])
        vareps = sb("vareps", [P, TILES])
        rstd = sb("rstd", [P, TILES])
        h = sb("h", [P, TILES, DM])
        hT = sb("hT", [P, DT, TILES * P])
        logits = sb("logits", [P, TILES, E])
        best = sb("best", [P, TILES, 8])
        best_i = sb("best_i", [P, TILES, 8], U32)
        best_f = sb("best_f", [P, TILES, 8])
        one_hot = sb("one_hot", [P, top, TILES, E])
        chosen = sb("chosen", [P, TILES, E], BF16)
        counts = sb("counts", [P, E])
        filled = sb("filled", [P, E, MOST])
        groups = sb("groups", [P, E])
        upto = [sb(f"upto{n}", [P, E]) for n in range(4)]
        base = sb("base", [P, E])
        place = sb("place", [P, TILES, E])
        picked = sb("picked", [P, top, TILES, E])
        slot_f = sb("slot_f", [P, top, TILES])
        passed = sb("passed", [P, GROUPS, E])
        expert_f = sb("expert_f", [P, GROUPS])
        expert_c = sb("expert_c", [P, GROUPS])
        margin = sb("margin", [P, TILES])
        TB = [bank(f"TB{n}") for n in range(4)]
        LG = bank("LG")
        RK = bank("RK")
        CN = bank("CN")
        s_load = sem("load")
        s_zset = sem("zset")
        s_zero = sem("zeroed")
        s_const = sem("const")
        s_dv = sem("dve_steps")
        s_mom = sem("moments")
        s_veps = sem("vareps")
        s_rstd = sem("rstd")
        s_h = sem("h")
        s_tr = sem("transposed")
        s_tc = sem("hT")
        s_lg = sem("logits")
        s_ch = sem("chosen")
        s_rk = sem("ranks")
        s_cn = sem("counts")
        s_mg = sem("margin")
        s_wt = sem("weights")
        s_slot = sem("slots")
        s_sc = sem("scattered")
        loads = [(router[:, :, :], w["router"].rearrange("(k p) e -> p k e", p=P)), (prefix_f[:, :], w["prefix"]),
                 (iota[:, :], w["iota"])]
        if "router_b" in w:
            loads += [(rbias[:, :], w["router_b"].unsqueeze(0).broadcast_to([P, E]))]
        LOADED = 16 * len(loads)
        block = ctx.enter_context(nc.Block())

        @block.sync
        def _(sp):
            for dst, src in loads:
                sp.dma_start(dst, src).then_inc(s_load, 16)
            sp.wait_ge(s_zset, 1)
            zv = xs_rows.rearrange("(z p r) n -> z p (r n)", p=P, r=ZW // DM)
            for z in range(ZDMAS):
                sp.dma_start(zv[z], zeros[:, :]).then_inc(s_zero, 16)

        @block.gpsimd
        def _(pool):
            pool.memset(zeros[:, :], 0.0).then_inc(s_zset, 1)
            pool.wait_ge(s_mom, TILES)
            pool.tensor_tensor(vareps[:, :], mv[:, :, 1], consts["ln_eps"][:, :], ALU.add).then_inc(s_veps, 1)
            pool.wait_ge(s_veps, 1)
            pool.tensor_tensor(rstd[:, :], vareps[:, :], consts["mhalf"][:, :], ALU.pow).then_inc(s_rstd, 1)
            pool.wait_ge(s_zero, 16 * ZDMAS)
            pool.wait_ge(s_h, TILES)
            pool.wait_ge(s_slot, 1)
            for k in range(top):
                for T in range(TILES):
                    pool.indirect_dma_start(out=xs_rows, out_offset=bass.IndirectOffsetOnAxis(ap=slot_u[:, k, T:T + 1], axis=0),
                                            in_=h[:, T, :], in_offset=None).then_inc(s_sc, 16)
            pool.wait_ge(s_sc, 16 * top * TILES)

        @block.vector
        def _(dve):
            steps = [0]

            def step(ins):
                steps[0] += 1
                ins.then_inc(s_dv, 1)
                dve.wait_ge(s_dv, steps[0])

            for T in range(TILES):
                last = dve.bn_stats(stats[:, T, :], x[:, T, :])
                if T == TILES - 1:
                    step(last)
            for T in range(TILES):
                dve.bn_aggr(mv[:, T, :], stats[:, T, :]).then_inc(s_mom, 1)
            dve.memset(ones[:, :], 1.0).then_inc(s_const, 1)
            dve.wait_ge(s_load, LOADED)
            dve.tensor_copy(prefix[:, :], prefix_f[:, :]).then_inc(s_const, 1)
            dve.wait_ge(s_rstd, 1)
            for T in range(TILES):
                dve.tensor_scalar(h[:, T, :], x[:, T, :], mv[:, T, 0:1], rstd[:, T:T + 1], ALU.subtract, ALU.mult)\
                   .then_inc(s_h, 1)
            dve.wait_ge(s_lg, 1)
            lg = LG[:, 0:TILES * E].rearrange("p (t e) -> p t e", e=E)
            if "router_b" in w:
                step(dve.tensor_tensor(logits[:, :, :], lg, rbias[:, :].unsqueeze(1).broadcast_to([P, TILES, E]), ALU.add))
            else:
                step(dve.tensor_copy(logits[:, :, :], lg))
            for T in range(TILES):
                last = dve.max(best[:, T, :], logits[:, T, :])
            step(last)
            for T in range(TILES):
                last = dve.max_index(best_i[:, T, :], best[:, T, :], logits[:, T, :])
            step(last)
            if top == 2:
                dve.tensor_tensor(margin[:, :], best[:, :, 0], best[:, :, 1], ALU.subtract).then_inc(s_mg, 1)
            step(dve.tensor_copy(best_f[:, :, :], best_i[:, :, :]))
            io = iota[:, 0:E].unsqueeze(1).broadcast_to([P, TILES, E])
            for k in range(top):
                last = dve.tensor_tensor(one_hot[:, k, :, :], io, best_f[:, :, k:k + 1].broadcast_to([P, TILES, E]),
                                         ALU.is_equal)
            step(last)
            if top == 2:
                dve.tensor_tensor(chosen[:, :, :], one_hot[:, 0, :, :], one_hot[:, 1, :, :], ALU.add).then_inc(s_ch, 1)
            else:
                dve.tensor_copy(chosen[:, :, :], one_hot[:, 0, :, :]).then_inc(s_ch, 1)
            dve.wait_ge(s_cn, 1)
            step(dve.tensor_scalar(counts[:, :], CN[:, 0:E], 1.0 / GR, None, ALU.mult))
            step(dve.tensor_tensor(filled[:, :, :], counts[:, :].unsqueeze(2).broadcast_to([P, E, MOST]),
                                   iota[:, 0:MOST].unsqueeze(1).broadcast_to([P, E, MOST]), ALU.is_gt))
            step(dve.reduce_sum(groups[:, :], filled[:, :, :], AXX))
            step(dve.tensor_copy(upto[0][:, :], groups[:, :]))
            for n, by in enumerate((1, 2, 4)):
                dve.tensor_copy(upto[n + 1][:, 0:by], upto[n][:, 0:by])
                step(dve.tensor_tensor(upto[n + 1][:, by:E], upto[n][:, by:E], upto[n][:, 0:E - by], ALU.add))
            last_group = upto[3]
            step(dve.tensor_tensor(base[:, :], last_group[:, :], groups[:, :], ALU.subtract))
            step(dve.tensor_scalar(base[:, :], base[:, :], float(GR), None, ALU.mult))
            step(dve.tensor_tensor(passed[:, :, :], last_group[:, :].unsqueeze(1).broadcast_to([P, GROUPS, E]),
                                   iota[:, 0:GROUPS].unsqueeze(2).broadcast_to([P, GROUPS, E]), ALU.is_le))
            step(dve.reduce_sum(expert_f[:, :], passed[:, :, :], AXX))
            step(dve.tensor_scalar(expert_c[:, :], expert_f[:, :], float(E - 1), None, ALU.min))
            step(dve.tensor_copy(expert_i[:, :], expert_c[:, :]))
            dve.wait_ge(s_rk, 1)
            step(dve.tensor_tensor(place[:, :, :], RK[:, 0:TILES * E].rearrange("p (t e) -> p t e", e=E),
                                   base[:, :].unsqueeze(1).broadcast_to([P, TILES, E]), ALU.add))
            for k in range(top):
                step(dve.tensor_tensor(picked[:, k, :, :], place[:, :, :], one_hot[:, k, :, :], ALU.mult))
                step(dve.reduce_sum(slot_f[:, k, :], picked[:, k, :, :], AXX))
            dve.tensor_copy(slot_u[:, :, :], slot_f[:, :, :]).then_inc(s_slot, 1)

        @block.scalar
        def _(act):
            for u in range(TILES // 2):
                act.wait_ge(s_tr, u + 1)
                act.activation(hT[:, :, u * SEQ:(u + 1) * SEQ], TB[u % 4][:, :].rearrange("p (d s) -> p d s", d=DT), ACT.Copy)\
                   .then_inc(s_tc, 1)
            if top == 2:
                act.wait_ge(s_mg, 1)
                act.activation(weight[:, 0, :], margin[:, :], ACT.Sigmoid).then_inc(s_wt, 1)
                act.activation(weight[:, 1, :], margin[:, :], ACT.Sigmoid, scale=-1.0).then_inc(s_wt, 1)

        @block.tensor
        def _(pe):
            for u in range(TILES // 2):
                pe.wait_ge(s_h, 2 * u + 2)
                if u >= 4:
                    pe.wait_ge(s_tc, u - 3)
                for d in range(DT):
                    for t in range(TT):
                        c = d * SEQ + t * P
                        last = pe.transpose(TB[u % 4][:, c:c + P], h[:, 2 * u + t, d * P:(d + 1) * P], ident[:, :])
                last.then_inc(s_tr, 1)
            pe.wait_ge(s_load, LOADED)
            for T in range(TILES):
                pe.wait_ge(s_tc, T // 2 + 1)
                for kk in range(DT):
                    last = pe.matmul(LG[:, T * E:(T + 1) * E], hT[:, kk, T * P:(T + 1) * P], router[:, kk, :],
                                     start=(kk == 0), stop=(kk == DT - 1))
            last.then_inc(s_lg, 1)
            pe.wait_ge(s_const, 2)
            pe.wait_ge(s_ch, 1)
            for T in range(TILES):
                last = pe.matmul(CN[:, 0:E], ones[:, :], chosen[:, T, :], start=(T == 0), stop=(T == TILES - 1))
            last.then_inc(s_cn, 1)
            ch = chosen[:, :, :].rearrange("p t e -> p (t e)")
            W = TILES * E
            pe.matmul(RK[:, 0:W], prefix[:, :], ch, start=True, stop=False, skip_group_check=True)
            for d in range(1, TILES):
                last = pe.matmul(RK[:, d * E:W], ones[:, :], ch[:, 0:W - d * E], start=False, stop=(d == TILES - 1),
                                 skip_group_check=True)
            last.then_inc(s_rk, 1)


def combine_rows(nc, name, x, top, ys_rows, slot_u, weight):
    QUARTERS = 4
    with ExitStack() as ctx:
        sc = Scope(nc, ctx, name + "c")
        got = sc.sb("got", [P, top, TILES, DM])
        s_got = [sc.sem(f"got{n}") for n in range(QUARTERS)]
        s_sum = sc.sem("sum")
        PER = TILES // QUARTERS
        block = ctx.enter_context(nc.Block())

        @block.gpsimd
        def _(pool):
            for T in range(TILES):
                for k in range(top):
                    pool.indirect_dma_start(out=got[:, k, T, :], out_offset=None, in_=ys_rows,
                                            in_offset=bass.IndirectOffsetOnAxis(ap=slot_u[:, k, T:T + 1], axis=0))\
                        .then_inc(s_got[T // PER], 16)

        @block.vector
        def _(dve):
            for T in range(TILES):
                dve.wait_ge(s_got[T // PER], 16 * top * PER)
                if top == 1:
                    dve.tensor_tensor(x[:, T, :], got[:, 0, T, :], x[:, T, :], ALU.add).then_inc(s_sum, 1)
                else:
                    for k in range(top):
                        if k:
                            dve.wait_ge(s_sum, T * top + k)
                        dve.scalar_tensor_tensor(x[:, T, :], got[:, k, T, :], weight[:, k, T:T + 1], x[:, T, :],
                                                 ALU.mult, ALU.add).then_inc(s_sum, 1)
            dve.wait_ge(s_sum, TILES * top)


def build(nc, t, out):
    Scope.taken.clear()
    with ExitStack() as ctx:
        x = ctx.enter_context(nc.sbuf_tensor("x", [P, TILES, DM], F32))
        consts = {"ident": ctx.enter_context(nc.sbuf_tensor("ident", [P, P], F32)),
                  "ident_bf": ctx.enter_context(nc.sbuf_tensor("ident_bf", [P, P], BF16)),
                  "mhalf": ctx.enter_context(nc.sbuf_tensor("mhalf", [P, TILES], F32)),
                  "ln_eps": ctx.enter_context(nc.sbuf_tensor("ln_eps", [P, TILES], F32)),
                  "ret_eps": ctx.enter_context(nc.sbuf_tensor("ret_eps", [P, TILES], F32))}
        retention_layer(nc, "ret", x, consts, {
            "x": t["x"], "wq": t["L0_attn_Wq"], "wk": t["L0_attn_Wk"], "wv": t["L0_attn_Wv"], "wg": t["L0_attn_Wg"],
            "wo": t["L0_attn_Wo"], "bo": t["L0_attn_bo"], "bg": t["L0_attn_bg"], "gamma": t["L0_attn_ln_gamma"],
            "beta": t["L0_attn_ln_beta"], "qdec": t["qdec"], "kdec": t["kdec"], "keep": t["keep"],
            "ident": t["ident"], "mhalf": t["mhalf"], "ln_eps": t["ln_eps"], "ret_eps": t["ret_eps"]})
        if STAGES >= 2:
            bf16_identity(nc, consts)
            attention_layer(nc, "x0", x, consts, {
                "wq": t["L0_xattn_Wq"], "wk": t["L0_xattn_Wk"], "wv": t["L0_xattn_Wv"], "wo": t["L0_xattn_Wo"],
                "bq": t["L0_xattn_bq"], "bk": t["L0_xattn_bk"], "bv": t["L0_xattn_bv"], "bo": t["L0_xattn_bo"],
                "ctxT": t["ctxT"], "mask": t["mask"]}, dh=16, cross=True, masked=True, causal=False)
        if STAGES >= 3:
            expert_layer(nc, "e0", x, consts, {
                "router": t["L0_ffn_router_w"], "router_b": t["L0_ffn_router_b"], "w1": t["L0_ffn_w1"],
                "b1": t["L0_ffn_b1"], "w2": t["L0_ffn_w2"], "b2": t["L0_ffn_b2"], "prefix": t["prefix"],
                "iota": t["iota"]}, top=1, hidden=1024)
            Scope.clear_semaphores(nc)
        if STAGES >= 4:
            attention_layer(nc, "a1", x, consts, {
                "wq": t["L1_attn_Wq"], "wk": t["L1_attn_Wk"], "wv": t["L1_attn_Wv"], "wo": t["L1_attn_Wo"],
                "bo": t["L1_attn_bo"], "cosx": t["cosx"], "sinx": t["sinx"], "causal": t["causal"]},
                dh=64, cross=False, masked=False, causal=True)
        if STAGES >= 5:
            attention_layer(nc, "x1", x, consts, {
                "wq": t["L1_xattn_w_q"], "wk": t["L1_xattn_w_k"], "wv": t["L1_xattn_w_v"], "wo": t["L1_xattn_w_o"],
                "bq": t["L1_xattn_b_q"], "bk": t["L1_xattn_b_k"], "bv": t["L1_xattn_b_v"], "bo": t["L1_xattn_b_o"],
                "ctxT": t["ctxT"]}, dh=16, cross=True, masked=False, causal=False)
        if STAGES >= 6:
            expert_layer(nc, "e1", x, consts, {
                "router": t["L1_ffn_router_w"], "gate": t["L1_ffn_gate_proj"], "up": t["L1_ffn_up_proj"],
                "down": t["L1_ffn_down_proj"], "prefix": t["prefix"], "iota": t["iota"]}, top=2, hidden=704)
        s_store = ctx.enter_context(nc.semaphore("store"))
        with nc.Block() as block:
            @block.sync
            def _(sp):
                sp.dma_start(out.rearrange("b (t p) n -> p (b t) n", p=P), x[:, :, :]).then_inc(s_store, 16)
                sp.wait_ge(s_store, 16)


def bf16_identity(nc, consts):
    with nc.semaphore("identbf") as s_id, nc.Block() as block:
        @block.vector
        def _(dve):
            dve.tensor_copy(consts["ident_bf"][:, :], consts["ident"][:, :]).then_inc(s_id, 1)
            dve.wait_ge(s_id, 1)



def kernel(**inputs):
    import numpy as np
    import concourse.bacc as bacc
    from concourse.bass_utils import run_bass_kernel_spmd as run

    nc = bacc.Bacc("TRN2", target_bir_lowering=False, num_devices=1)
    arrays = {}

    def slots(wt):
        p = np.zeros((wt.shape[0], HEADS, 32), wt.dtype)
        p[:, :, 0:16] = np.asarray(wt).reshape(wt.shape[0], HEADS, 16)
        return p.reshape(wt.shape[0], HEADS * 32)

    def cols(b, width):
        return np.asarray(b).reshape(-1, width).T

    for k, v in inputs.items():
        v = np.asarray(v)
        if k in ("L0_attn_Wq", "L0_attn_Wk", "L0_xattn_Wq", "L0_xattn_Wk"):
            v = slots(v)
        elif k in ("L1_xattn_w_q", "L1_xattn_w_k"):
            v = slots(v.T)
        elif k in ("L1_xattn_w_v", "L1_xattn_w_o"):
            v = v.T
        elif k in ("L0_xattn_bq", "L0_xattn_bk", "L1_xattn_b_q", "L1_xattn_b_k"):
            v = cols(slots(v[None, :]), P)
        elif k in ("L0_xattn_bv", "L1_xattn_b_v"):
            v = cols(v, P)
        elif k == "L0_ffn_b1":
            v = v.reshape(8, -1, P).transpose(0, 2, 1)
        elif k == "mask_SxS2_bk1":
            k = "mask"
        elif k == "ctx_1024":
            k, v = "ctxT", v.transpose(2, 0, 1).reshape(DM, BATCH * SEQ)
        arrays[k] = np.ascontiguousarray(v)

    arrays["ident"] = np.eye(P, dtype=np.float32)
    arrays["mhalf"] = np.full((P, TILES), -0.5, np.float32)
    arrays["ln_eps"] = np.full((P, TILES), LN_EPS, np.float32)
    arrays["ret_eps"] = np.full((P, TILES), RET_EPS, np.float32)
    gam = 1.0 - 2.0 ** (-5.0 - np.arange(HEADS, dtype=np.float64))
    tpos = np.arange(SEQ, dtype=np.float64)
    qd = (gam[:, None] ** tpos[None, :]) * 0.25
    kd = gam[:, None] ** (-tpos[None, :])
    head_of = 4 * np.arange(4)[None, :] + (np.arange(P) // 32)[:, None]
    arrays["qdec"] = qd[head_of].astype(np.float32)
    arrays["kdec"] = kd[head_of].astype(np.float32)
    tri = (np.arange(P)[None, :] >= np.arange(P)[:, None]).astype(np.float32)
    arrays["keep"] = np.concatenate([tri, np.ones((P, P), np.float32), tri], 1)
    late = np.where(np.arange(SEQ)[None, None, :] > (np.arange(P)[:, None, None] + P * np.arange(TT)[None, :, None]), NEG, 0.0)
    arrays["causal"] = late.astype(np.float32)
    inv = (1.0 / np.float32(10000.0) ** (np.arange(0, 64, 2, dtype=np.float32) / np.float32(64))).astype(np.float32)
    ang = (np.arange(SEQ, dtype=np.float32)[:, None] * inv[None, :]).astype(np.float32)
    cos = np.cos(ang.astype(np.float64)).reshape(TT, P, 32).transpose(1, 0, 2)
    sin = np.sin(ang.astype(np.float64)).reshape(TT, P, 32).transpose(1, 0, 2)
    c2 = np.repeat(cos, 2, axis=-1)
    s2 = np.concatenate([-sin, sin], -1)
    arrays["cosx"] = np.stack([c2 * 0.125, c2], 1).astype(np.float32)
    arrays["sinx"] = np.stack([s2 * 0.125, s2], 1).astype(np.float32)
    arrays["prefix"] = (np.arange(P)[:, None] < np.arange(P)[None, :]).astype(np.float32)
    arrays["iota"] = np.broadcast_to(np.arange(32, dtype=np.float32), (P, 32)).copy()

    t = {n: nc.dram_tensor(f"in_{n}", a.shape, mybir.dt.from_np(a.dtype), kind="ExternalInput").ap()
         for n, a in arrays.items()}
    out = nc.dram_tensor("out_0", (BATCH, SEQ, DM), F32, kind="ExternalOutput").ap()
    build(nc, t, out)
    r = run(nc, [{f"in_{n}": a for n, a in arrays.items()}], core_ids=[0])
    return r.results[0]["out_0"]
```

```python
import concourse.bass as bass
from concourse import mybir
from contextlib import ExitStack

F32 = mybir.dt.float32
F32R = mybir.dt.float32r
BF16 = mybir.dt.bfloat16
U32 = mybir.dt.uint32
I32 = mybir.dt.int32
U8 = mybir.dt.uint8
ALU = mybir.AluOpType
ACT = mybir.ActivationFunctionType
AXX = mybir.AxisListType.X
ds = bass.ds

STAGES = 6
P = 128
BATCH = 8
SEQ = 256
DM = 256
TT = SEQ // P
DT = DM // P
TILES = BATCH * TT
HEADS = 16
NEG = -1.0e30
LN_EPS = 1e-5
RET_EPS = 1e-3
BANK = 512


def await_ge(eng, sem, value):
    if not (isinstance(value, int) and value <= 0):
        eng.wait_ge(sem, value)


def seq_steps(eng, step):
    step(0, 0, True, True, False)
    with eng.Fori(0, (BATCH - 2) // 2) as i:
        step(i * 2 + 1, 1, True, True, True)
        step(i * 2 + 2, 0, True, True, True)
    step(BATCH - 1, 1, False, True, True)
    step(BATCH, 0, False, False, True)


class Scope:

    taken = []

    def __init__(self, nc, ctx, name):
        self.nc, self.ctx, self.name = nc, ctx, name

    def sb(self, name, shape, dt=F32):
        return self.ctx.enter_context(self.nc.sbuf_tensor(f"{self.name}_{name}", shape, dt))

    def bank(self, name):
        return self.ctx.enter_context(self.nc.psum_tensor(f"{self.name}_{name}", [P, BANK], F32))

    def sem(self, name):
        s = self.nc.alloc_semaphore(f"{self.name}_{name}")
        Scope.taken.append(s)
        return s

    @staticmethod
    def clear_semaphores(nc):
        nc.all_engine_barrier()
        nc.clear_and_free_semaphores(list(Scope.taken))
        Scope.taken.clear()
        nc.all_engine_barrier()


def attention_layer(nc, name, x, consts, w, dh, cross, masked, causal):
    rope = not cross
    DI = HEADS * dh
    DIT = DI // P
    HPT = P // dh
    G = 2 * HPT
    NG = HEADS // G
    PAIR = dh == 16
    ROWS = 32 if PAIR else dh
    BACK_SLOTS = 6
    XB_SLOT = 5
    SC = float(dh) ** -0.5
    ident, ident_bf = consts["ident"], consts["ident_bf"]

    if cross:
        USES = [("hT", 0, "act", 3, 0), ("q", 0, "act", 5, 0), ("k", 0, "act", 7, 0), ("v", 0, "act", 10, 0)]
    else:
        USES = [("hT", 0, "act", 2, 0), ("qr", 0, "dve", 3, 0), ("qr", 1, "dve", 4, 0), ("qr", 2, "dve", 5, 0),
                ("qr", 3, "dve", 6, 0), ("kr", 0, "dve", 7, 0), ("v", 0, "act", 7, 1), ("kr", 1, "dve", 8, 0),
                ("kr", 2, "dve", 9, 0), ("v", 1, "act", 9, 1), ("kr", 3, "dve", 10, 0), ("v", 2, "act", 11, 1),
                ("qT", 0, "act", 11, 0), ("qT", 1, "act", 12, 0), ("qT", 2, "act", 12, 1), ("v", 3, "act", 13, 1),
                ("qT", 3, "act", 13, 0), ("kT", 0, "act", 14, 0), ("kT", 1, "act", 14, 1), ("kT", 2, "act", 15, 0),
                ("kT", 3, "act", 15, 1)]
    NF = len(USES)
    ACT_PER = {"hT": 1, "q": 2, "k": 4, "v": 2 if cross else 1, "qT": 1, "kT": 1}
    DVE_PER = 3

    def emptied(b, j):
        e = USES[j][2]
        per = [(ACT_PER[u[0]] if e == "act" else DVE_PER) for u in USES if u[2] == e]
        upto = [(ACT_PER[u[0]] if e == "act" else DVE_PER) for u in USES[:j + 1] if u[2] == e]
        return e, b * sum(per) + sum(upto)

    with ExitStack() as ctx:
        sc = Scope(nc, ctx, name)
        sb, bank, sem = sc.sb, sc.bank, sc.sem
        wq = sb("wq", [P, DT, DI])
        wk = sb("wk", [P, DT, DI])
        wv = sb("wv", [P, DT, DI])
        wo = sb("wo", [P, DIT, DM])
        bo = sb("bo", [P, DM])
        if cross:
            cT = [sb(f"cT{n}", [P, DT, SEQ]) for n in range(2)]
            bq = sb("bq", [P, DIT])
            bqs = sb("bqs", [P, DIT])
            bk = sb("bk", [P, DIT, 2])
            bv = sb("bv", [P, DIT])
        stats = sb("stats", [P, TT, 6])
        mv = sb("mv", [P, TT, 2])
        vareps = sb("vareps", [P, TT])
        rstd = sb("rstd", [P, TT])
        h = sb("h", [P, TT, DM])
        hT = sb("hT", [P, DT, SEQ])
        KH = 2 if PAIR else 1
        VW = 32 if PAIR else dh
        QT = [sb(f"QT{n}", [P, DIT, SEQ]) for n in range(2)]
        KT = [sb(f"KT{n}", [P, DIT, KH, SEQ]) for n in range(2)]
        V = [sb(f"V{n}", [P, TT, HEADS, VW]) for n in range(2)]
        negmax = sb("negmax", [P, 4, TT])
        bias = sb("bias", [P, 4, TT]) if masked else negmax
        PR = [sb(f"PR{n}", [P, TT, SEQ]) for n in range(2)]
        PN = [sb(f"PN{n}", [P, TT, SEQ]) for n in range(2)]
        PT = [sb(f"PT{n}", [P, TT, SEQ]) for n in range(2)]
        rowsum = sb("rowsum", [P, 4, TT])
        rowinv = sb("rowinv", [P, 4, TT])
        AOT = sb("AOT", [P, DIT, SEQ])
        if rope:
            cosx = sb("cosx", [P, 2, TT, dh])
            sinx = sb("sinx", [P, 2, TT, dh])
            RA = [sb(f"RA{n}", [P, BANK]) for n in range(2)]
            RB = [sb(f"RB{n}", [P, BANK]) for n in range(2)]
            QKR = [sb(f"QKR{n}", [P, TT, DI]) for n in range(2)]
        if masked:
            mask_u8 = sb("mask_u8", [P, TT, SEQ], U8)
            mask_f = sb("mask_f", [P, TT, SEQ])
            allmasked = sb("allmasked", [P, TT])
            anykey = sb("anykey", [P, TT])
        if masked or causal:
            maskneg = sb("maskneg", [P, TT, SEQ], BF16)
        if causal:
            maskneg_f = sb("maskneg_f", [P, TT, SEQ])

        SCO = [bank(f"SCO{n}") for n in range(2)]
        TRP = [bank(f"TRP{n}") for n in range(2)]
        O = [bank(f"O{n}") for n in range(2)]
        FB = bank("FB")
        BB = bank("BB")
        FBS = [FB, BB]

        s_load = sem("load")
        s_setup = sem("setup")
        s_ctx = [sem(f"ctx{n}") for n in range(2)]
        s_maskf = sem("maskf")
        s_stats = sem("stats")
        s_tick = sem("tick")
        s_mom = sem("moments")
        s_veps = sem("vareps")
        s_rstd = sem("rstd")
        s_h = sem("h")
        s_xb = sem("xb")
        s_ff = sem("front_filled")
        s_fa = sem("front_act")
        s_fd = sem("front_dve")
        s_rope = sem("rope")
        s_sc = sem("scores")
        s_nm = sem("negmax")
        s_mx = sem("bias") if masked else s_nm
        s_ex = sem("exp")
        s_tr = sem("transposed")
        s_pt = sem("ptcopied")
        s_rc = sem("rowinv")
        s_pn = sem("normalised")
        s_av = sem("av")
        s_oe = sem("oevac")
        s_out = sem("outproj")
        s_x = sem("xdone")

        loads = [(wq[:, :, :], w["wq"].rearrange("(k p) n -> p k n", p=P)),
                 (wk[:, :, :], w["wk"].rearrange("(k p) n -> p k n", p=P)),
                 (wv[:, :, :], w["wv"].rearrange("(k p) n -> p k n", p=P)),
                 (wo[:, :, :], w["wo"].rearrange("(k p) n -> p k n", p=P)),
                 (bo[:, :], w["bo"].unsqueeze(0).broadcast_to([P, DM]))]
        if cross:
            loads += [(bq[:, :], w["bq"]), (bk[:, :, :], w["bk"]), (bv[:, :], w["bv"])]
        if rope:
            loads += [(cosx[:, :, :, :], w["cosx"]), (sinx[:, :, :, :], w["sinx"])]
        if masked:
            loads += [(mask_u8[:, :, :], w["mask"].rearrange("(t p) s -> p t s", p=P))]
        if causal:
            loads += [(maskneg_f[:, :, :], w["causal"])]
        LOADED = 16 * len(loads)
        NORM_PER = TT if causal else 1
        SETUP = (4 if PAIR else 0) + (1 if cross else 0) + (2 if masked else 0) + (1 if causal else 0)

        block = ctx.enter_context(nc.Block())

        @block.sync
        def _(sp):
            for dst, src in loads:
                sp.dma_start(dst, src).then_inc(s_load, 16)
            if cross:
                ctx_v = w["ctxT"].rearrange("(k p) n -> p k n", p=P)
                for b in range(2):
                    sp.dma_start(cT[b][:, :, :], ctx_v[:, :, b * SEQ:(b + 1) * SEQ]).then_inc(s_ctx[b], 16)
                with sp.Fori(1, BATCH // 2) as i:
                    for n in range(2):
                        sp.wait_ge(s_ff, i * (2 * NF) + NF * (n - 1))
                        sp.dma_start(cT[n][:, :, :], ctx_v[:, :, ds(i * (2 * SEQ) + n * SEQ, SEQ)])\
                          .then_inc(s_ctx[n], 16)

        @block.gpsimd
        def _(pool):
            def front(k, b):
                if k == (1 if cross else 0):
                    pool.wait_ge(s_mom, b * 2 + 2)
                    pool.tensor_tensor(vareps[:, :], mv[:, :, 1], consts["ln_eps"][:, 0:TT], ALU.add).then_inc(s_veps, 1)
                    pool.wait_ge(s_veps, b + 1)
                    pool.tensor_tensor(rstd[:, :], vareps[:, :], consts["mhalf"][:, 0:TT], ALU.pow).then_inc(s_rstd, 1)
                if k == XB_SLOT:
                    pool.wait_ge(s_h, b * 2 + 2)
                    for t in range(TT):
                        xt = x[:, ds(b * 2 + t, 1), :].rearrange("p a n -> p (a n)")
                        pool.tensor_tensor(xt, xt, bo[:, :], ALU.add).then_inc(s_xb, 1)
                for j, (kind, n, e, slot, fb) in enumerate(USES):
                    if e == "dve" and slot == k:
                        pool.wait_ge(s_fd, emptied(b, j)[1])
                        t, c = n // 2, n % 2
                        pool.tensor_tensor(QKR[0 if kind == "qr" else 1][:, t, c * BANK:(c + 1) * BANK], RA[n % 2][:, :],
                                           RB[n % 2][:, :], ALU.add).then_inc(s_rope, 1)

            def normalise(s, k):
                g = s * HEADS + k
                pool.wait_ge(s_rc, g + 1)
                await_ge(pool, s_tr, g - 1)
                inv = rowinv[:, k % 4, :]
                if causal:
                    for t in range(TT):
                        W = P * (t + 1)
                        pool.tensor_tensor(PN[k % 2][:, t, 0:W], PR[k % 2][:, t, 0:W], inv[:, t:t + 1].broadcast_to([P, W]),
                                           ALU.mult).then_inc(s_pn, 1)
                else:
                    pool.tensor_tensor(PN[k % 2][:, :, :], PR[k % 2][:, :, :],
                                       inv.unsqueeze(2).broadcast_to([P, TT, SEQ]), ALU.mult).then_inc(s_pn, 1)

            def step(s, par, front_, heads, back):
                for k in range(HEADS if heads else BACK_SLOTS):
                    if front_:
                        front(k, s + 1)
                    if heads:
                        normalise(s, k)

            pool.wait_ge(s_load, LOADED)
            for k in range(HEADS):
                front(k, 0)
            seq_steps(pool, step)

        @block.vector
        def _(dve):
            dve.wait_ge(s_load, LOADED)
            n_setup = 0
            dve.sem_inc(s_x, 1)
            if PAIR:
                for n in range(2):
                    for e in range(2):
                        vz = V[n][:, :, :, :].rearrange("p t (g e) d -> p (t g) e d", e=2)
                        dve.memset(vz[:, :, e, dh * (1 - e):dh * (2 - e)], 0.0).then_inc(s_setup, 1)
                        n_setup += 1
            if cross:
                dve.tensor_scalar(bqs[:, :], bq[:, :], SC, None, ALU.mult).then_inc(s_setup, 1)
                n_setup += 1
            if masked:
                dve.tensor_copy(mask_f[:, :, :], mask_u8[:, :, :]).then_inc(s_maskf, 1)
                dve.wait_ge(s_maskf, 1)
                dve.tensor_scalar(maskneg[:, :, :], mask_f[:, :, :], NEG, None, ALU.mult).then_inc(s_setup, 1)
                dve.tensor_reduce(allmasked[:, :], mask_f[:, :, :], AXX, ALU.min).then_inc(s_maskf, 1)
                dve.wait_ge(s_maskf, 2)
                dve.tensor_scalar(anykey[:, :], allmasked[:, :], -1.0, 1.0, ALU.mult, ALU.add).then_inc(s_setup, 1)
                n_setup += 2
            if causal:
                dve.tensor_copy(maskneg[:, :, :], maskneg_f[:, :, :]).then_inc(s_setup, 1)
                n_setup += 1
            assert n_setup == SETUP

            def front(k, b):
                if k == 0:
                    for t in range(TT):
                        dve.bn_stats(stats[:, t, :], x[:, ds(b * 2 + t, 1), :].rearrange("p a n -> p (a n)"))\
                           .then_inc(s_stats, 1)
                    dve.wait_ge(s_stats, b * 2 + 2)
                    dve.sem_inc(s_tick, 1)
                    for t in range(TT):
                        dve.bn_aggr(mv[:, t, :], stats[:, t, :]).then_inc(s_mom, 1)
                if k == (2 if cross else 1):
                    dve.wait_ge(s_rstd, b + 1)
                    await_ge(dve, s_ff, (b - 1) * NF + 1)
                    for t in range(TT):
                        dve.tensor_scalar(h[:, t, :], x[:, ds(b * 2 + t, 1), :].rearrange("p a n -> p (a n)"),
                                          mv[:, t, 0:1], rstd[:, t:t + 1], ALU.subtract, ALU.mult).then_inc(s_h, 1)
                for j, (kind, n, e, slot, fb) in enumerate(USES):
                    if e == "dve" and slot == k:
                        which = 0 if kind == "qr" else 1
                        t = n // 2
                        dve.wait_ge(s_ff, b * NF + j + 1)
                        await_ge(dve, s_rope, b * 8 + 4 * which + n - 1)
                        A = RA[n % 2][:, :].rearrange("p (h d) -> p h d", d=dh)
                        Bv = RB[n % 2][:, :].rearrange("p (h i two) -> p h i two", i=dh // 2, two=2)
                        q = FBS[fb][:, :].rearrange("p (h d) -> p h d", d=dh)
                        q2 = FBS[fb][:, :].rearrange("p (h i two) -> p h i two", i=dh // 2, two=2)
                        nh = BANK // dh
                        cos = cosx[:, which, t, :].unsqueeze(1).broadcast_to([P, nh, dh])
                        sn = [sinx[:, which, t, i * dh // 2:(i + 1) * dh // 2].unsqueeze(1).broadcast_to([P, nh, dh // 2])
                              for i in range(2)]
                        dve.tensor_tensor(A, q, cos, ALU.mult).then_inc(s_fd, 1)
                        dve.tensor_tensor(Bv[:, :, :, 0], q2[:, :, :, 1],
                                          sn[0], ALU.mult).then_inc(s_fd, 1)
                        dve.tensor_tensor(Bv[:, :, :, 1], q2[:, :, :, 0],
                                          sn[1], ALU.mult).then_inc(s_fd, 1)

            def step(s, par, front_, heads, back):
                for k in range(HEADS if heads else BACK_SLOTS):
                    g = s * HEADS + k
                    if front_ and cross:
                        front(k, s + 1)
                    if heads:
                        dve.wait_ge(s_sc, g + 1)
                        dve.reduce_max(negmax[:, k % 4, :], SCO[k % 2][:, :].rearrange("p (t s) -> p t s", t=TT),
                                       AXX, negate=True).then_inc(s_nm, 1)
                        if masked:
                            dve.wait_ge(s_nm, g + 1)
                            dve.tensor_tensor(bias[:, k % 4, :], negmax[:, k % 4, :], anykey[:, :], ALU.mult)\
                               .then_inc(s_mx, 1)
                    if (heads and k >= 1) or (k == 0 and back):
                        pk = (k - 1) % 4
                        dve.wait_ge(s_ex, g * 2)
                        dve.reciprocal(rowinv[:, pk, :], rowsum[:, pk, :]).then_inc(s_rc, 1)
                    if (heads and k >= 2) or (k < 2 and back):
                        pk = k % 2
                        dve.wait_ge(s_tr, g - 1)
                        await_ge(dve, s_av, g - 3)
                        W = 3 * P if causal else TT * SEQ
                        dve.tensor_copy(PT[pk][:, :, :].rearrange("p a b -> p (a b)")[:, 0:W], TRP[pk][:, 0:W])\
                           .then_inc(s_pt, 1)
                    if front_ and rope:
                        front(k, s + 1)
                    if back and k == 5:
                        dve.wait_ge(s_out, s + 1)
                        dve.wait_ge(s_xb, s * 2)
                        xs = x[:, ds(s * 2 - 2, 2), :].rearrange("p a n -> p (a n)")
                        dve.tensor_tensor(xs, BB[:, :], xs, ALU.add).then_inc(s_x, 1)

            for k in range(HEADS):
                front(k, 0)
            seq_steps(dve, step)
            dve.wait_ge(s_x, BATCH + 1)

        @block.scalar
        def _(act):
            act.wait_ge(s_load, LOADED)
            act.wait_ge(s_setup, SETUP)

            def front(k, b, par):
                for j, (kind, n, e, slot, fb) in enumerate(USES):
                    if e != "act" or slot != k:
                        continue
                    act.wait_ge(s_ff, b * NF + j + 1)
                    if kind == "hT":
                        act.activation(hT[:, :, :].rearrange("p a b -> p (a b)"), FBS[fb][:, :], ACT.Copy).then_inc(s_fa, 1)
                    if kind == "q":
                        for i in range(DIT):
                            act.activation(QT[par][:, i, :], FBS[fb][:, i * SEQ:(i + 1) * SEQ], ACT.Identity,
                                           bias=bqs[:, i:i + 1], scale=SC).then_inc(s_fa, 1)
                    if kind == "k":
                        for i in range(DIT):
                            for e in range(2):
                                act.activation(KT[par][:, i, e, :], FBS[fb][:, i * SEQ:(i + 1) * SEQ], ACT.Identity,
                                               bias=bk[:, i, e:e + 1], scale=consts["parity"][:, e:e + 1]).then_inc(s_fa, 1)
                    if kind in ("qT", "kT"):
                        dst = QT[par][:, 2 * n:2 * n + 2, :] if kind == "qT" else KT[par][:, 2 * n:2 * n + 2, 0, :]
                        act.activation(dst.rearrange("p a b -> p (a b)"), FBS[fb][:, :], ACT.Copy).then_inc(s_fa, 1)
                    if kind == "v" and cross:
                        for e in range(2):
                            dst = V[par][:, :, :, :].rearrange("p t (g e) d -> p (t g) e d", e=2)[:, :, e, dh * e:dh * (e + 1)]
                            src = FBS[fb][:, :].rearrange("p (g e d) -> p g e d", e=2, d=dh)[:, :, e, :]
                            act.activation(dst, src, ACT.Copy).then_inc(s_fa, 1)
                    if kind == "v" and not cross:
                        t, c = n // 2, n % 2
                        act.activation(V[par][:, t, 8 * c:8 * c + 8, :], FBS[fb][:, :].rearrange("p (h d) -> p h d", d=dh),
                                       ACT.Copy).then_inc(s_fa, 1)

            def outputs_copy(s, par, q):
                act.wait_ge(s_av, s * HEADS + G * (q + 1))
                act.wait_ge(s_out, s + 1)
                for i in range(2):
                    src = O[(par * NG + q) % 2][:, i * SEQ:(i + 1) * SEQ]
                    if cross:
                        act.activation(AOT[:, 2 * q + i, :], src, ACT.Identity, bias=bv[:, 2 * q + i:2 * q + i + 1])\
                           .then_inc(s_oe, 1)
                    else:
                        act.activation(AOT[:, 2 * q + i, :], src, ACT.Copy).then_inc(s_oe, 1)

            def step(s, par, front_, heads, back):
                for k in range(HEADS if heads else BACK_SLOTS):
                    g = s * HEADS + k
                    if heads:
                        act.wait_ge(s_mx, g + 1)
                        await_ge(act, s_pn, g * NORM_PER - NORM_PER)
                        for t in range(TT):
                            W = P * (t + 1) if causal else SEQ
                            act.activation(PR[k % 2][:, t, 0:W], SCO[k % 2][:, t * SEQ:t * SEQ + W], ACT.Exp,
                                           bias=bias[:, k % 4, t:t + 1],
                                           scale=anykey[:, t:t + 1] if masked else 1.0,
                                           accum_out=rowsum[:, k % 4, t:t + 1]).then_inc(s_ex, 1)
                    if front_:
                        front(k, s + 1, 1 - par)
                    for q in range(NG):
                        slot = G * (q + 1) + 2
                        if slot < HEADS and heads and k == slot:
                            outputs_copy(s, par, q)
                        if slot >= HEADS and back and k == slot - HEADS:
                            outputs_copy(s - 1, 1 - par, q)

            for k in range(HEADS):
                front(k, 0, 0)
            seq_steps(act, step)

        @block.tensor
        def _(pe):
            pe.wait_ge(s_load, LOADED)
            pe.wait_ge(s_setup, SETUP)
            pe.sem_inc(s_out, 1)

            def front(k, b, par):
                for j, (kind, n, _, slot, fb) in enumerate(USES):
                    if slot != k:
                        continue
                    if j == 0:
                        pe.wait_ge(s_h, b * 2 + 2)
                    before = [i for i in range(j) if USES[i][4] == fb]
                    if before:
                        e, v = emptied(b, before[-1])
                        pe.wait_ge(s_fa if e == "act" else s_fd, v)
                    elif fb == 0:
                        e, v = emptied(b - 1, max(i for i in range(NF) if USES[i][4] == 0))
                        await_ge(pe, s_fa if e == "act" else s_fd, v)
                    else:
                        await_ge(pe, s_x, b)
                    if kind == "hT":
                        for d in range(DT):
                            for t in range(TT):
                                c = d * SEQ + t * P
                                last = pe.transpose(FBS[fb][:, c:c + P], h[:, t, d * P:(d + 1) * P], ident[:, :])
                    if cross and kind in ("k", "v"):
                        pe.wait_ge(s_ctx[par], b * 8 + 16 - 8 * par)
                    if kind in ("q", "k"):
                        wt = wq if kind == "q" else wk
                        for i in range(2):
                            m = 2 * n + i
                            for kk in range(DT):
                                rhs = hT[:, kk, :] if kind == "q" else cT[par][:, kk, :]
                                last = pe.matmul(FBS[fb][:, i * SEQ:(i + 1) * SEQ], wt[:, kk, m * P:(m + 1) * P], rhs,
                                                 start=(kk == 0), stop=(kk == DT - 1))
                    if kind in ("qr", "kr", "v") and not cross:
                        wt = {"qr": wq, "kr": wk, "v": wv}[kind]
                        t, c = n // 2, n % 2
                        for kk in range(DT):
                            last = pe.matmul(FBS[fb][:, :], hT[:, kk, t * P:(t + 1) * P], wt[:, kk, c * BANK:(c + 1) * BANK],
                                             start=(kk == 0), stop=(kk == DT - 1))
                    if kind == "v" and cross:
                        for t in range(TT):
                            for kk in range(DT):
                                last = pe.matmul(FBS[fb][:, t * DI:(t + 1) * DI], cT[par][:, kk, t * P:(t + 1) * P],
                                                 wv[:, kk, :], start=(kk == 0), stop=(kk == DT - 1))
                    if kind in ("qT", "kT"):
                        which = 0 if kind == "qT" else 1
                        pe.wait_ge(s_rope, b * 8 + 4 * (which + 1))
                        for i in range(2):
                            for t in range(TT):
                                m = 2 * n + i
                                last = pe.transpose(FBS[fb][:, i * SEQ + t * P:i * SEQ + (t + 1) * P],
                                                    QKR[which][:, t, m * P:(m + 1) * P], ident[:, :])
                    last.then_inc(s_ff, 1)

            def scores(s, k, par):
                g = s * HEADS + k
                if k == 0:
                    pe.wait_ge(s_fa, emptied(s, NF - 1)[1])
                await_ge(pe, s_ex, g * 2 - 2)
                bank_ = SCO[k % 2]
                tile, r = k // HPT, ROWS * ((k % HPT) // KH)
                add_mask = masked or causal
                for t in range(TT):
                    W = P * (t + 1) if causal else SEQ
                    last = pe.matmul(bank_[:, t * SEQ:t * SEQ + W], QT[par][r:r + ROWS, tile, t * P:(t + 1) * P],
                                     KT[par][r:r + ROWS, tile, k % KH, 0:W], start=(t == 0 or not add_mask),
                                     stop=not add_mask, skip_group_check=add_mask)
                if add_mask:
                    last = pe.matmul(bank_[:, :], ident_bf[:, :], maskneg[:, :, :].rearrange("p t s -> p (t s)"),
                                     start=False, stop=True, skip_group_check=True)
                last.then_inc(s_sc, 1)

            def transposes(g, k):
                pe.wait_ge(s_pn, g * NORM_PER + NORM_PER)
                await_ge(pe, s_pt, g - 1)
                for st in range(TT):
                    for t in range(TT):
                        if causal and st > t:
                            continue
                        c = st * SEQ + t * P if not causal else (2 * P if st else t * P)
                        last = pe.transpose(TRP[k % 2][:, c:c + P], PN[k % 2][:, t, st * P:(st + 1) * P], ident[:, :])
                last.then_inc(s_tr, 1)

            def av(s, g, k, par):
                pe.wait_ge(s_pt, g + 1)
                q = k // G
                if k % G == 0:
                    await_ge(pe, s_oe, (s * NG + q - 1) * 2)
                r = ROWS * ((k % HPT) // KH)
                c = (k % G) // HPT * SEQ
                o = O[(par * NG + q) % 2]
                for st in range(TT):
                    first = st == 0 and k % KH == 0
                    final = st == TT - 1 and k % KH == KH - 1
                    if causal and st:
                        o_cols, p_cols = slice(c + P, c + SEQ), slice(2 * P, 3 * P)
                    else:
                        o_cols, p_cols = slice(c, c + SEQ), slice(st * SEQ, (st + 1) * SEQ)
                    last = pe.matmul(o[r:r + ROWS, o_cols], V[par][:, st, k, :],
                                     PT[k % 2][:, :, :].rearrange("p a b -> p (a b)")[:, p_cols],
                                     start=first, stop=final, skip_group_check=True)
                last.then_inc(s_av, 1)

            def step(s, par, front_, heads, back):
                for k in range(HEADS if heads else BACK_SLOTS):
                    g = s * HEADS + k
                    if heads:
                        scores(s, k, par)
                    if (heads and k >= 2) or (k < 2 and back):
                        transposes(g - 2, (k - 2) % HEADS)
                    if heads and k >= 3:
                        av(s, g - 3, k - 3, par)
                    if k < 3 and back:
                        av(s - 1, g - 3, k + HEADS - 3, 1 - par)
                    if front_:
                        front(k, s + 1, 1 - par)
                    if back and k == 4:
                        pe.wait_ge(s_oe, s * NG * 2)
                        pe.wait_ge(s_x, s)
                        for t in range(TT):
                            for kk in range(DIT):
                                last = pe.matmul(BB[:, t * DM:(t + 1) * DM], AOT[:, kk, t * P:(t + 1) * P], wo[:, kk, :],
                                                 start=(kk == 0), stop=(kk == DIT - 1))
                        last.then_inc(s_out, 1)

            for k in range(HEADS):
                front(k, 0, 0)
            seq_steps(pe, step)


def retention_layer(nc, name, x, consts, w):
    dh = 16
    HPT = P // dh
    ROWS = 32
    PTW = 3 * P
    RING = 4
    ident = consts["ident"]
    USES = [("hT", 0, "act", 3), ("q", 0, "dve", 5), ("k", 0, "dve", 7), ("v", 0, "act", 9), ("g", 0, "dve", 11)]
    PER = {"hT": 1, "q": 1, "k": 2, "v": 2, "g": 1}
    NF = len(USES)
    BACK_STEPS = 13

    def emptied(b, j):
        e = USES[j][2]
        per = sum(PER[u[0]] for u in USES if u[2] == e)
        return e, b * per + sum(PER[u[0]] for u in USES[:j + 1] if u[2] == e)

    with ExitStack() as ctx:
        sc = Scope(nc, ctx, name)
        sb, bank, sem = sc.sb, sc.bank, sc.sem
        wq = sb("wq", [P, DT, DM])
        wk = sb("wk", [P, DT, DM])
        wv = sb("wv", [P, DT, DM])
        wg = sb("wg", [P, DT, DM])
        wo = sb("wo", [P, DT, DM])
        bo = sb("bo", [P, DM])
        bg = sb("bg", [P, DM])
        lng = sb("lng", [P, DM])
        lnb = sb("lnb", [P, DM])
        qdec = sb("qdec", [P, DT, SEQ])
        kdec = sb("kdec", [P, 2, DT, SEQ])
        keep = sb("keep", [P, PTW])
        stats = sb("stats", [P, TT, 6])
        mv = sb("mv", [P, TT, 2])
        vareps = sb("vareps", [P, TT])
        rstd = sb("rstd", [P, TT])
        h = sb("h", [P, TT, DM])
        hT = sb("hT", [P, DT, SEQ])
        QT = [sb(f"QT{n}", [P, DT, SEQ]) for n in range(2)]
        KT = [sb(f"KT{n}", [P, 2, DT, SEQ]) for n in range(2)]
        V = [sb(f"V{n}", [P, TT, HEADS, ROWS]) for n in range(2)]
        gate = sb("gate", [P, TT, DM])
        th = sb("th", [P, TT, DM])
        swish2 = [sb(f"swish2_{n}", [P, TT, DM]) for n in range(2)]
        PT = [sb(f"PT{n}", [P, PTW]) for n in range(RING)]
        OT = sb("OT", [P, DT, SEQ])
        stats2 = sb("stats2", [P, TT, 6])
        mv2 = sb("mv2", [P, TT, 2])
        vareps2 = sb("vareps2", [P, TT])
        rstd2 = sb("rstd2", [P, TT])
        Y = sb("Y", [P, TT, DM])
        YT = sb("YT", [P, DT, SEQ])

        SCO = [bank(f"SCO{n}") for n in range(RING)]
        O = [bank(f"O{n}") for n in range(2)]
        FB = bank("FB")
        BB = bank("BB")

        s_load = sem("load")
        s_xload = sem("xload")
        s_stats = sem("stats")
        s_tick = sem("tick")
        s_mom = sem("moments")
        s_veps = sem("vareps")
        s_rstd = sem("rstd")
        s_h = sem("h")
        s_xb = sem("xb")
        s_ff = sem("front_filled")
        s_fa = sem("front_act")
        s_fd = sem("front_dve")
        s_th = sem("tanh")
        s_sw = sem("swish")
        s_sc = sem("scores")
        s_pt = sem("pt")
        s_av = sem("av")
        s_setup = sem("setup")
        s_oe = sem("oevac")
        s_ot = sem("o_transposed")
        s_st2 = sem("stats2")
        s_mom2 = sem("moments2")
        s_veps2 = sem("vareps2")
        s_rstd2 = sem("rstd2")
        s_y1 = sem("y_normed")
        s_y2 = sem("y_scaled")
        s_y3 = sem("y_shifted")
        s_y4 = sem("y_gated")
        s_yt = sem("y_transposed")
        s_ya = sem("yT")
        s_out = sem("outproj")
        s_x = sem("xdone")

        loads = [(t[:, :, :], w[n].rearrange("(k p) n -> p k n", p=P))
                 for t, n in ((wq, "wq"), (wk, "wk"), (wv, "wv"), (wg, "wg"), (wo, "wo"))]
        loads += [(t[:, :], w[n].unsqueeze(0).broadcast_to([P, DM]))
                  for t, n in ((bo, "bo"), (bg, "bg"), (lng, "gamma"), (lnb, "beta"))]
        loads += [(qdec[:, :, :], w["qdec"]), (kdec[:, :, :, :], w["kdec"]), (keep[:, :], w["keep"])]
        loads += [(consts["ident"][:, :], w["ident"]), (consts["mhalf"][:, :], w["mhalf"]),
                  (consts["parity"][:, :], w["parity"]), (consts["ln_eps"][:, :], w["ln_eps"]), (consts["ret_eps"][:, :], w["ret_eps"])]
        LOADED = 16 * len(loads)
        x_v = w["x"].rearrange("b (t p) n -> p (b t) n", p=P)

        block = ctx.enter_context(nc.Block())

        @block.sync
        def _(sp):
            sp.dma_start(x[:, :, :], x_v).then_inc(s_xload, 16)
            for dst, src in loads:
                sp.dma_start(dst, src).then_inc(s_load, 16)

        @block.gpsimd
        def _(pool):
            pool.wait_ge(s_load, LOADED)

            def front(b):
                pool.wait_ge(s_mom, b * 2 + 2)
                pool.tensor_tensor(vareps[:, :], mv[:, :, 1], consts["ln_eps"][:, 0:TT], ALU.add).then_inc(s_veps, 1)
                pool.wait_ge(s_veps, b + 1)
                pool.tensor_tensor(rstd[:, :], vareps[:, :], consts["mhalf"][:, 0:TT], ALU.pow).then_inc(s_rstd, 1)
                pool.wait_ge(s_h, b * 2 + 2)
                for t in range(TT):
                    xt = x[:, ds(b * 2 + t, 1), :].rearrange("p a n -> p (a n)")
                    pool.tensor_tensor(xt, xt, bo[:, :], ALU.add).then_inc(s_xb, 1)

            def back_norm(b):
                pool.wait_ge(s_mom2, b * 2 + 2)
                pool.tensor_tensor(vareps2[:, :], mv2[:, :, 1], consts["ret_eps"][:, 0:TT], ALU.add).then_inc(s_veps2, 1)
                pool.wait_ge(s_veps2, b + 1)
                pool.tensor_tensor(rstd2[:, :], vareps2[:, :], consts["mhalf"][:, 0:TT], ALU.pow).then_inc(s_rstd2, 1)

            def back_affine(b):
                for t in range(TT):
                    pool.wait_ge(s_y1, b * 2 + t + 2)
                    pool.tensor_tensor(Y[:, t, :], Y[:, t, :], lng[:, :], ALU.mult).then_inc(s_y2, 1)
                for t in range(TT):
                    pool.wait_ge(s_y2, b * 2 + t + 1)
                    pool.tensor_tensor(Y[:, t, :], Y[:, t, :], lnb[:, :], ALU.add).then_inc(s_y3, 1)

            def step(s, par, front_, heads, back):
                if front_:
                    front(s + 1)
                if back:
                    back_norm(s - 1)
                    back_affine(s - 1)

            front(0)
            seq_steps(pool, step)

        @block.vector
        def _(dve):
            dve.sem_inc(s_x, 1)
            dve.sem_inc(s_y1, 1)
            for n in range(2):
                for e in range(2):
                    vz = V[n][:, :, :, :].rearrange("p t (g e) d -> p (t g) e d", e=2)
                    dve.memset(vz[:, :, e, dh * (1 - e):dh * (2 - e)], 0.0).then_inc(s_setup, 1)
            dve.wait_ge(s_xload, 16)
            dve.wait_ge(s_load, LOADED)

            def front(k, b, par):
                if k == 0:
                    for t in range(TT):
                        dve.bn_stats(stats[:, t, :], x[:, ds(b * 2 + t, 1), :].rearrange("p a n -> p (a n)"))\
                           .then_inc(s_stats, 1)
                    dve.wait_ge(s_stats, b * 2 + 2)
                    dve.sem_inc(s_tick, 1)
                    for t in range(TT):
                        dve.bn_aggr(mv[:, t, :], stats[:, t, :]).then_inc(s_mom, 1)
                if k == 2:
                    dve.wait_ge(s_rstd, b + 1)
                    await_ge(dve, s_ff, (b - 1) * NF + 1)
                    for t in range(TT):
                        dve.tensor_scalar(h[:, t, :], x[:, ds(b * 2 + t, 1), :].rearrange("p a n -> p (a n)"),
                                          mv[:, t, 0:1], rstd[:, t:t + 1], ALU.subtract, ALU.mult).then_inc(s_h, 1)
                for j, (kind, n, e, slot) in enumerate(USES):
                    if slot != k or e != "dve":
                        continue
                    dve.wait_ge(s_ff, b * NF + j + 1)
                    if kind == "q":
                        dve.tensor_tensor(QT[par][:, :, :].rearrange("p a b -> p (a b)"), FB[:, :],
                                          qdec[:, :, :].rearrange("p a b -> p (a b)"), ALU.mult).then_inc(s_fd, 1)
                    if kind == "k":
                        for e in range(2):
                            dve.tensor_tensor(KT[par][:, e, :, :].rearrange("p a b -> p (a b)"), FB[:, :],
                                              kdec[:, e, :, :].rearrange("p a b -> p (a b)"), ALU.mult).then_inc(s_fd, 1)
                    if kind == "g":
                        dve.tensor_tensor(gate[:, :, :], FB[:, :].rearrange("p (t n) -> p t n", t=TT),
                                          bg[:, :].unsqueeze(1).broadcast_to([P, TT, DM]), ALU.add).then_inc(s_fd, 1)
                if k == 15:
                    dve.wait_ge(s_th, b + 1)
                    dve.scalar_tensor_tensor(swish2[par][:, :, :], th[:, :, :], 1.0, gate[:, :, :], ALU.add, ALU.mult)\
                       .then_inc(s_sw, 1)

            def back_part(k, b, par):
                if k == 3:
                    dve.wait_ge(s_ot, b + 2)
                    for t in range(TT):
                        dve.bn_stats(stats2[:, t, :], BB[:, t * DM:(t + 1) * DM]).then_inc(s_st2, 1)
                    dve.wait_ge(s_st2, b * 2 + 2)
                    dve.sem_inc(s_tick, 1)
                    for t in range(TT):
                        dve.bn_aggr(mv2[:, t, :], stats2[:, t, :]).then_inc(s_mom2, 1)
                if k == 5:
                    dve.wait_ge(s_rstd2, b + 1)
                    for t in range(TT):
                        dve.tensor_scalar(Y[:, t, :], BB[:, t * DM:(t + 1) * DM], mv2[:, t, 0:1], rstd2[:, t:t + 1],
                                          ALU.subtract, ALU.mult).then_inc(s_y1, 1)
                if k == 8:
                    dve.wait_ge(s_sw, b + 1)
                    for t in range(TT):
                        dve.wait_ge(s_y3, b * 2 + t + 1)
                        dve.scalar_tensor_tensor(Y[:, t, :], Y[:, t, :], 0.5, swish2[par][:, t, :], ALU.mult, ALU.mult)\
                           .then_inc(s_y4, 1)
                if k == 12:
                    dve.wait_ge(s_out, b + 2)
                    dve.wait_ge(s_xb, b * 2 + 2)
                    xs = x[:, ds(b * 2, 2), :].rearrange("p a n -> p (a n)")
                    dve.tensor_tensor(xs, BB[:, :], xs, ALU.add).then_inc(s_x, 1)

            def step(s, par, front_, heads, back):
                for k in range(HEADS if heads else BACK_STEPS):
                    g = s * HEADS + k
                    if front_:
                        front(k, s + 1, 1 - par)
                    if heads:
                        dve.wait_ge(s_sc, g + 1)
                        await_ge(dve, s_av, g - RING + 1)
                        dve.tensor_tensor(PT[k % RING][:, :], SCO[k % RING][:, 0:PTW], keep[:, :], ALU.mult)\
                           .then_inc(s_pt, 1)
                    if back:
                        back_part(k, s - 1, 1 - par)

            for k in range(HEADS):
                front(k, 0, 0)
            seq_steps(dve, step)
            dve.wait_ge(s_x, BATCH + 1)

        @block.scalar
        def _(act):
            def front(k, b, par):
                for j, (kind, n, e, slot) in enumerate(USES):
                    if e != "act" or slot != k:
                        continue
                    act.wait_ge(s_ff, b * NF + j + 1)
                    if kind == "hT":
                        act.activation(hT[:, :, :].rearrange("p a b -> p (a b)"), FB[:, :], ACT.Copy).then_inc(s_fa, 1)
                    else:
                        for e in range(2):
                            dst = V[par][:, :, :, :].rearrange("p t (g e) d -> p (t g) e d", e=2)[:, :, e, dh * e:dh * (e + 1)]
                            src = FB[:, :].rearrange("p (g e d) -> p g e d", e=2, d=dh)[:, :, e, :]
                            act.activation(dst, src, ACT.Copy).then_inc(s_fa, 1)
                if k == 13:
                    act.wait_ge(s_fd, emptied(b, NF - 1)[1])
                    await_ge(act, s_sw, b)
                    act.activation(th[:, :, :], gate[:, :, :], ACT.Tanh, scale=0.5).then_inc(s_th, 1)

            def back_part(k, b, par):
                if k == 1:
                    act.wait_ge(s_av, b * HEADS + HEADS)
                    act.wait_ge(s_ot, b + 1)
                    act.activation(OT[:, :, :].rearrange("p a b -> p (a b)"), O[par][:, :], ACT.Copy).then_inc(s_oe, 1)
                if k == 10:
                    act.wait_ge(s_yt, b + 1)
                    act.wait_ge(s_out, b + 1)
                    act.activation(YT[:, :, :].rearrange("p a b -> p (a b)"), BB[:, :], ACT.Copy).then_inc(s_ya, 1)

            def step(s, par, front_, heads, back):
                for k in range(HEADS if heads else BACK_STEPS):
                    if back:
                        back_part(k, s - 1, 1 - par)
                    if front_:
                        front(k, s + 1, 1 - par)

            for k in range(HEADS):
                front(k, 0, 0)
            seq_steps(act, step)

        @block.tensor
        def _(pe):
            pe.sem_inc(s_out, 1)
            pe.sem_inc(s_ot, 1)
            pe.wait_ge(s_setup, 4)
            pe.wait_ge(s_load, LOADED)

            def front(k, b, par):
                for j, (kind, n, _, slot) in enumerate(USES):
                    if slot != k:
                        continue
                    if j == 0:
                        e, v = emptied(b - 1, NF - 1)
                        pe.wait_ge(s_h, b * 2 + 2)
                    else:
                        e, v = emptied(b, j - 1)
                    await_ge(pe, s_fa if e == "act" else s_fd, v)
                    if kind == "hT":
                        for d in range(DT):
                            for t in range(TT):
                                c = d * SEQ + t * P
                                last = pe.transpose(FB[:, c:c + P], h[:, t, d * P:(d + 1) * P], ident[:, :])
                    if kind in ("q", "k"):
                        wt = wq if kind == "q" else wk
                        for i in range(2):
                            for kk in range(DT):
                                last = pe.matmul(FB[:, i * SEQ:(i + 1) * SEQ], wt[:, kk, i * P:(i + 1) * P],
                                                 hT[:, kk, :], start=(kk == 0), stop=(kk == DT - 1))
                    if kind in ("v", "g"):
                        wt = wv if kind == "v" else wg
                        for t in range(TT):
                            for kk in range(DT):
                                last = pe.matmul(FB[:, t * DM:(t + 1) * DM], hT[:, kk, t * P:(t + 1) * P],
                                                 wt[:, kk, :], start=(kk == 0), stop=(kk == DT - 1))
                    last.then_inc(s_ff, 1)

            def scores(s, k, par):
                g = s * HEADS + k
                if k == 0:
                    pe.wait_ge(s_fa, emptied(s, 3)[1])
                    pe.wait_ge(s_fd, emptied(s, 2)[1])
                await_ge(pe, s_pt, g - RING + 1)
                tile, r, e = k // HPT, ROWS * ((k % HPT) // 2), k % 2
                for st in range(TT):
                    last = pe.matmul(SCO[k % RING][:, st * SEQ:st * SEQ + SEQ - st * P],
                                     KT[par][r:r + ROWS, e, tile, st * P:(st + 1) * P],
                                     QT[par][r:r + ROWS, tile, st * P:SEQ], start=True, stop=True)
                last.then_inc(s_sc, 1)

            def av(s, g, k, par):
                pe.wait_ge(s_pt, g + 1)
                if k == 0:
                    await_ge(pe, s_oe, s - 1)
                r, c = ROWS * ((k % HPT) // 2), k // HPT * SEQ
                for st in range(TT):
                    last = pe.matmul(O[par][r:r + ROWS, c + st * P:c + SEQ], V[par][:, st, k, :],
                                     PT[k % RING][:, st * SEQ:st * SEQ + SEQ - st * P],
                                     start=(st == 0 and k % 2 == 0), stop=(st == TT - 1 and k % 2 == 1),
                                     skip_group_check=True)
                last.then_inc(s_av, 1)

            def back_part(k, b, par):
                if k == 2:
                    pe.wait_ge(s_oe, b + 1)
                    pe.wait_ge(s_x, b + 1)
                    for t in range(TT):
                        for d in range(DT):
                            last = pe.transpose(BB[:, t * DM + d * P:t * DM + (d + 1) * P], OT[:, d, t * P:(t + 1) * P],
                                                ident[:, :])
                    last.then_inc(s_ot, 1)
                if k == 10:
                    pe.wait_ge(s_y4, b * 2 + 2)
                    for d in range(DT):
                        for t in range(TT):
                            c = d * SEQ + t * P
                            last = pe.transpose(BB[:, c:c + P], Y[:, t, d * P:(d + 1) * P], ident[:, :])
                    last.then_inc(s_yt, 1)
                if k == 12:
                    pe.wait_ge(s_ya, b + 1)
                    for t in range(TT):
                        for kk in range(DT):
                            last = pe.matmul(BB[:, t * DM:(t + 1) * DM], YT[:, kk, t * P:(t + 1) * P], wo[:, kk, :],
                                             start=(kk == 0), stop=(kk == DT - 1))
                    last.then_inc(s_out, 1)

            def step(s, par, front_, heads, back):
                for k in range(HEADS if heads else BACK_STEPS):
                    g = s * HEADS + k
                    if heads:
                        scores(s, k, par)
                    if heads and k >= 2:
                        av(s, g - 2, k - 2, par)
                    if k < 2 and back:
                        av(s - 1, g - 2, k + HEADS - 2, 1 - par)
                    if front_:
                        front(k, s + 1, 1 - par)
                    if back:
                        back_part(k, s - 1, 1 - par)

            for k in range(HEADS):
                front(k, 0, 0)
            seq_steps(pe, step)


def expert_layer(nc, name, x, consts, w, top, hidden):
    E = 8
    ROWS = BATCH * SEQ
    GR = SEQ
    GROUPS = top * ROWS // GR + E
    SLOTS = GROUPS * GR
    MOST = ROWS // GR
    glu_bias = "b1" in w
    MT = [(m * P, min(P, hidden - m * P)) for m in range((hidden + P - 1) // P)]
    NM = len(MT)
    WHOLE = hidden // P
    REST = hidden - WHOLE * P
    ident = consts["ident"]
    xs_rows = nc.dram_tensor(f"{name}_sorted", (SLOTS, DM), F32).ap()
    ys_rows = nc.dram_tensor(f"{name}_outputs", (SLOTS, DM), F32).ap()

    with ExitStack() as outer:
        keep_ = Scope(nc, outer, name)
        slot_u = keep_.sb("slot_u", [P, top, TILES], U32)
        expert_i = keep_.sb("expert_i", [P, GROUPS], I32)
        weight = keep_.sb("weight", [P, top, TILES])
        route_rows(nc, name, x, consts, w, top, E, GR, GROUPS, MOST, xs_rows, slot_u, expert_i, weight)

        with ExitStack() as ctx:
            sc = Scope(nc, ctx, name + "m")
            sb, bank, sem = sc.sb, sc.bank, sc.sem
            LEAD = 3
            WU = [sb(f"WU{n}", [P, 2 * DT, hidden]) for n in range(2)]
            WD = [sb(f"WD{n}", [P, NM, DM]) for n in range(2)]
            WU_hi, WU_lo = (sb(f"WU_{part}", [P, 2 * DT, hidden], F32R) for part in ("hi", "lo"))
            WD_hi, WD_lo = (sb(f"WD_{part}", [P, NM, DM], F32R) for part in ("hi", "lo"))
            if glu_bias:
                B1 = [sb(f"B1{n}", [P, 2 * NM]) for n in range(2)]
                B2 = [sb(f"B2{n}", [P, DM]) for n in range(2)]
            XR = [sb(f"XR{n}", [P, TT, DM]) for n in range(2)]
            XT_hi, XT_lo = ([sb(f"XT_{part}{n}", [P, DT, SEQ], F32R) for n in range(2)] for part in ("hi", "lo"))
            SG = [sb(f"SG{n}", [P, SEQ]) for n in range(4)]
            H = [sb(f"H{n}", [P, SEQ]) for n in range(4)]
            H_hi, H_lo = ([sb(f"H_{part}{n}", [P, SEQ], F32R) for n in range(4)] for part in ("hi", "lo"))
            YS = [sb(f"YS{n}", [P, TT, DM]) for n in range(2)]
            U = [bank(f"U{n}") for n in range(4)]
            Y = [bank(f"Y{n}") for n in range(2)]
            XB = bank("XB")
            s_w = [sem(f"weights{n}") for n in range(2)]
            s_b = [sem(f"biases{n}") for n in range(2)]
            s_wuh = sem("up_weights_hi")
            s_wul = sem("up_weights_lo")
            s_wdh = sem("down_weights_hi")
            s_wdl = sem("down_weights_lo")
            s_xt = sem("x_transposed")
            s_xh = sem("xT_hi")
            s_xl = sem("xT_lo")
            s_up = sem("up")
            s_sg = sem("sigmoid")
            s_h = sem("hidden")
            s_hh = sem("hidden_hi")
            s_hl = sem("hidden_lo")
            s_dn = sem("down")
            s_ye = sem("y_out")
            s_ys = [sem(f"y_stored{n}") for n in range(2)]
            s_tick = sem("tick")
            s_stick = sem("sync_tick")
            W_DMAS = 4 + (1 if REST else 0)

            def groups(eng, group):
                group(0, 0, True, True)
                group(1, 1, False, True)
                with eng.Fori(1, GROUPS // 2 - 1) as i:
                    for n in range(2):
                        group(i * 2 + n, n, False, True)
                group(GROUPS - 2, 0, False, True)
                group(GROUPS - 1, 1, False, False)

            def arrived(g, n, dmas):
                return g * (8 * dmas) + 8 * dmas * (2 - n)

            def ring(n, m):
                return (m + NM * n) % 4

            def ahead(g, n, m, more):
                if m + LEAD < NM:
                    return g * NM + (m + LEAD), n, m + LEAD, g
                return (g * NM + (m + LEAD), 1 - n, m + LEAD - NM, g + 1) if more else None

            block = ctx.enter_context(nc.Block())

            @block.sync
            def _(sp):
                def load(g, n):
                    e = sp.value_load(expert_i[0:1, ds(g, 1)], min_val=0, max_val=E - 1)
                    if not (isinstance(g, int) and g < 2):
                        sp.wait_ge(s_wul, g * NM - NM)
                        sp.sem_inc(s_stick, 1)
                        sp.wait_ge(s_wdl, g * NM - NM)
                        sp.sem_inc(s_stick, 1)
                        sp.wait_ge(s_xt, g - 1)
                        sp.sem_inc(s_stick, 1)
                    if glu_bias:
                        w1 = w["w1"][ds(e, 1)].rearrange("a (k p) n -> p (a k) n", p=P)
                        up, gate = w1[:, :, 0:hidden], w1[:, :, hidden:2 * hidden]
                    else:
                        up = w["up"][ds(e, 1)].rearrange("a (k p) n -> p (a k) n", p=P)
                        gate = w["gate"][ds(e, 1)].rearrange("a (k p) n -> p (a k) n", p=P)
                    parts = [(WU[n][:, 0:DT, :], up), (WU[n][:, DT:2 * DT, :], gate)]
                    wd = w["w2" if glu_bias else "down"][ds(e, 1)].rearrange("a f n -> (a f) n")
                    parts += [(WD[n][:, 0:WHOLE, :], wd[0:WHOLE * P, :].rearrange("(m p) n -> p m n", p=P))]
                    if REST:
                        parts += [(WD[n][0:REST, WHOLE, :], wd[WHOLE * P:hidden, :])]
                    parts += [(XR[n][:, :, :], xs_rows[ds(g * GR, GR), :].rearrange("(t p) n -> p t n", p=P))]
                    assert len(parts) == W_DMAS
                    for dst, src in parts:
                        sp.dma_start(dst, src).then_inc(s_w[n], 16)
                    if glu_bias:
                        if not (isinstance(g, int) and g < 2):
                            sp.wait_ge(s_ye, g - 1)
                            sp.sem_inc(s_stick, 1)
                        sp.dma_start(B1[n][:, :], w["b1"][ds(e, 1)].rearrange("a p m -> p (a m)")).then_inc(s_b[n], 16)
                        sp.dma_start(B2[n][:, :], w["b2"][ds(e, 1), :].broadcast_to([P, DM])).then_inc(s_b[n], 16)
                load(0, 0)
                load(1, 1)
                with sp.Fori(1, GROUPS // 2) as i:
                    for n in range(2):
                        load(i * 2 + n, n)

            @block.gpsimd
            def _(pool):
                def split(f, n, m, g):
                    c, size = MT[m]
                    pool.wait_ge(s_wuh, f + 1)
                    pool.tensor_tensor(WU_lo[:, :, c:c + size], WU[n][:, :, c:c + size], WU_hi[:, :, c:c + size],
                                       ALU.subtract).then_inc(s_wul, 1)

                def store(g, n):
                    pool.wait_ge(s_ye, g + 1)
                    pool.sem_inc(s_tick, 1)
                    pool.dma_start(ys_rows[ds(g * GR, GR), :].rearrange("(t p) n -> p t n", p=P), YS[n][:, :, :])\
                        .then_inc(s_ys[n], 16)

                def group(g, n, first, more):
                    for m in range(NM):
                        tile = ahead(g, n, m, more)
                        if tile:
                            split(*tile)
                        if m == 3 and not first:
                            store(g - 1, 1 - n)

                for m in range(LEAD):
                    split(m, 0, m, 0)
                groups(pool, group)
                store(GROUPS - 1, 1)
                for n in range(2):
                    pool.wait_ge(s_ys[n], 16 * (GROUPS // 2))

            @block.tensor
            def _(pe):
                def x_transposes(g, n):
                    pe.wait_ge(s_w[n], arrived(g, n, W_DMAS))
                    await_ge(pe, s_xl, g)
                    for d in range(DT):
                        for t in range(TT):
                            c = d * SEQ + t * P
                            last = pe.transpose(XB[:, c:c + P], XR[n][:, t, d * P:(d + 1) * P], ident[:, :])
                    last.then_inc(s_xt, 1)

                def up(g, n, m):
                    c, size = MT[m]
                    if m == 0:
                        pe.wait_ge(s_xl, g + 1)
                    pe.wait_ge(s_wul, g * NM + (m + 1))
                    await_ge(pe, s_h, g * NM + (m - 3))
                    u = U[ring(n, m)]
                    for half in range(2):
                        out = u[0:size, half * SEQ:(half + 1) * SEQ]
                        for kk in range(DT):
                            hi = WU_hi[:, half * DT + kk, c:c + size]
                            lo = WU_lo[:, half * DT + kk, c:c + size]
                            pe.matmul(out, hi, XT_lo[n][:, kk, :], start=(kk == 0), stop=False)
                            pe.matmul(out, hi, XT_hi[n][:, kk, :], start=False, stop=False)
                            last = pe.matmul(out, lo, XT_hi[n][:, kk, :], start=False, stop=(kk == DT - 1))
                    last.then_inc(s_up, 1)

                def down(g, n, m):
                    size = MT[m][1]
                    pe.wait_ge(s_hl, g * NM + (m + 1))
                    pe.wait_ge(s_wdl, g * NM + (m + 1))
                    if m == 0:
                        await_ge(pe, s_ye, g - 1)
                    r = ring(n, m)
                    for t in range(TT):
                        out = Y[n][:, t * DM:(t + 1) * DM]
                        hi = H_hi[r][0:size, t * P:(t + 1) * P]
                        lo = H_lo[r][0:size, t * P:(t + 1) * P]
                        pe.matmul(out, lo, WD_hi[0:size, m, :], start=(m == 0 and t == 0), stop=False, skip_group_check=True)
                        pe.matmul(out, hi, WD_hi[0:size, m, :], start=False, stop=False, skip_group_check=True)
                        last = pe.matmul(out, hi, WD_lo[0:size, m, :], start=False, stop=(m == NM - 1),
                                         skip_group_check=True)
                    last.then_inc(s_dn, 1)

                def group(g, n, first, more):
                    for m in range(NM):
                        up(g, n, m)
                        if m >= 2:
                            down(g, n, m - 2)
                        elif not first:
                            down(g - 1, 1 - n, NM - 2 + m)
                        if m == 4 and more:
                            x_transposes(g + 1, 1 - n)

                x_transposes(0, 0)
                groups(pe, group)
                down(GROUPS - 1, 1, NM - 2)
                down(GROUPS - 1, 1, NM - 1)

            @block.scalar
            def _(act):
                def split(f, n, m, g):
                    c, size = MT[m]
                    if m == 0:
                        act.wait_ge(s_w[n], arrived(g, n, W_DMAS))
                    await_ge(act, s_dn, f - (NM - 1))
                    act.activation(WU_hi[:, :, c:c + size], WU[n][:, :, c:c + size], ACT.Copy).then_inc(s_wuh, 1)
                    act.activation(WD_hi[0:size, m, :], WD[n][0:size, m, :], ACT.Copy).then_inc(s_wdh, 1)

                def x_copy(g, n):
                    act.wait_ge(s_xt, g + 1)
                    act.activation(XT_hi[n][:, :, :].rearrange("p a b -> p (a b)"), XB[:, :], ACT.Copy).then_inc(s_xh, 1)

                def group(g, n, first, more):
                    if glu_bias:
                        act.wait_ge(s_b[n], arrived(g, n, 2))
                    for m in range(NM):
                        size = MT[m][1]
                        act.wait_ge(s_up, g * NM + (m + 1))
                        bias = B1[n][0:size, NM + m:NM + m + 1] if glu_bias else 0.0
                        act.activation(SG[ring(n, m)][0:size, :], U[ring(n, m)][0:size, SEQ:2 * SEQ],
                                       ACT.Sigmoid if glu_bias else ACT.Silu, bias=bias).then_inc(s_sg, 1)
                        tile = ahead(g, n, m, more)
                        if tile:
                            split(*tile)
                        if m == 4 and more:
                            x_copy(g + 1, 1 - n)

                for m in range(LEAD):
                    split(m, 0, m, 0)
                x_copy(0, 0)
                groups(act, group)

            @block.vector
            def _(dve):
                def split(f, n, m, g):
                    size = MT[m][1]
                    dve.wait_ge(s_wdh, f + 1)
                    dve.tensor_tensor(WD_lo[0:size, m, :], WD[n][0:size, m, :], WD_hi[0:size, m, :],
                                      ALU.subtract).then_inc(s_wdl, 1)

                def x_low(g, n):
                    dve.wait_ge(s_xh, g + 1)
                    dve.tensor_tensor(XT_lo[n][:, :, :].rearrange("p a b -> p (a b)"), XB[:, :],
                                      XT_hi[n][:, :, :].rearrange("p a b -> p (a b)"), ALU.subtract).then_inc(s_xl, 1)

                def y_copy(g, n):
                    dve.wait_ge(s_dn, g * NM + NM)
                    if not (isinstance(g, int) and g < 2):
                        dve.wait_ge(s_ys[n], g * 8 - 8 * n)
                    y = Y[n][:, :].rearrange("p (t n) -> p t n", t=TT)
                    if glu_bias:
                        dve.tensor_tensor(YS[n][:, :, :], y, B2[n][:, :].unsqueeze(1).broadcast_to([P, TT, DM]),
                                          ALU.add).then_inc(s_ye, 1)
                    else:
                        dve.tensor_copy(YS[n][:, :, :], y).then_inc(s_ye, 1)

                def group(g, n, first, more):
                    for m in range(NM):
                        size = MT[m][1]
                        r = ring(n, m)
                        dve.wait_ge(s_sg, g * NM + (m + 1))
                        await_ge(dve, s_dn, g * NM + (m - 3))
                        a = U[r][0:size, 0:SEQ]
                        if glu_bias:
                            dve.scalar_tensor_tensor(H[r][0:size, :], a, B1[n][0:size, m:m + 1], SG[r][0:size, :],
                                                     ALU.add, ALU.mult).then_inc(s_h, 1)
                        else:
                            dve.tensor_tensor(H[r][0:size, :], a, SG[r][0:size, :], ALU.mult).then_inc(s_h, 1)
                        tile = ahead(g, n, m, more)
                        if tile:
                            split(*tile)
                        dve.wait_ge(s_h, g * NM + (m + 1))
                        dve.tensor_copy(H_hi[r][0:size, :], H[r][0:size, :]).then_inc(s_hh, 1)
                        dve.wait_ge(s_hh, g * NM + (m + 1))
                        dve.tensor_tensor(H_lo[r][0:size, :], H[r][0:size, :], H_hi[r][0:size, :],
                                          ALU.subtract).then_inc(s_hl, 1)
                        if m == 4 and more:
                            x_low(g + 1, 1 - n)
                        if m == 2 and not first:
                            y_copy(g - 1, 1 - n)

                for m in range(LEAD):
                    split(m, 0, m, 0)
                x_low(0, 0)
                groups(dve, group)
                y_copy(GROUPS - 1, 1)

        combine_rows(nc, name, x, top, ys_rows, slot_u, weight)


def route_rows(nc, name, x, consts, w, top, E, GR, GROUPS, MOST, xs_rows, slot_u, expert_i, weight):
    ZW = 2048
    SLOTS = GROUPS * GR
    ZDMAS = SLOTS * DM // (P * ZW)
    ident = consts["ident"]
    with ExitStack() as ctx:
        sc = Scope(nc, ctx, name + "r")
        sb, bank, sem = sc.sb, sc.bank, sc.sem
        zeros = sb("zeros", [P, ZW])
        router = sb("router", [P, DT, E])
        if "router_b" in w:
            rbias = sb("rbias", [P, E])
        prefix_f = sb("prefix_f", [P, P])
        prefix = sb("prefix", [P, P], BF16)
        ones = sb("ones", [P, P], BF16)
        iota = sb("iota", [P, 32])
        stats = sb("stats", [P, TILES, 6])
        mv = sb("mv", [P, TILES, 2])
        vareps = sb("vareps", [P, TILES])
        rstd = sb("rstd", [P, TILES])
        h = sb("h", [P, TILES, DM])
        hT = sb("hT", [P, DT, TILES * P])
        logits = sb("logits", [P, TILES, E])
        best = sb("best", [P, TILES, 8])
        best_i = sb("best_i", [P, TILES, 8], U32)
        best_f = sb("best_f", [P, TILES, 8])
        one_hot = sb("one_hot", [P, top, TILES, E])
        chosen = sb("chosen", [P, TILES, E], BF16)
        counts = sb("counts", [P, E])
        filled = sb("filled", [P, E, MOST])
        groups = sb("groups", [P, E])
        upto = [sb(f"upto{n}", [P, E]) for n in range(4)]
        base = sb("base", [P, E])
        place = sb("place", [P, TILES, E])
        picked = sb("picked", [P, top, TILES, E])
        slot_f = sb("slot_f", [P, top, TILES])
        passed = sb("passed", [P, GROUPS, E])
        expert_f = sb("expert_f", [P, GROUPS])
        expert_c = sb("expert_c", [P, GROUPS])
        margin = sb("margin", [P, TILES])
        TB = [bank(f"TB{n}") for n in range(4)]
        LG = bank("LG")
        RK = bank("RK")
        CN = bank("CN")
        s_load = sem("load")
        s_zset = sem("zset")
        s_zero = sem("zeroed")
        s_const = sem("const")
        s_dv = sem("dve_steps")
        s_mom = sem("moments")
        s_veps = sem("vareps")
        s_rstd = sem("rstd")
        s_h = sem("h")
        s_tr = sem("transposed")
        s_tc = sem("hT")
        s_lg = sem("logits")
        s_ch = sem("chosen")
        s_rk = sem("ranks")
        s_cn = sem("counts")
        s_mg = sem("margin")
        s_wt = sem("weights")
        s_slot = sem("slots")
        s_sc = sem("scattered")
        loads = [(router[:, :, :], w["router"].rearrange("(k p) e -> p k e", p=P)), (prefix_f[:, :], w["prefix"]),
                 (iota[:, :], w["iota"])]
        if "router_b" in w:
            loads += [(rbias[:, :], w["router_b"].unsqueeze(0).broadcast_to([P, E]))]
        LOADED = 16 * len(loads)
        block = ctx.enter_context(nc.Block())

        @block.sync
        def _(sp):
            for dst, src in loads:
                sp.dma_start(dst, src).then_inc(s_load, 16)
            sp.wait_ge(s_zset, 1)
            zv = xs_rows.rearrange("(z p r) n -> z p (r n)", p=P, r=ZW // DM)
            for z in range(ZDMAS):
                sp.dma_start(zv[z], zeros[:, :]).then_inc(s_zero, 16)

        @block.gpsimd
        def _(pool):
            pool.memset(zeros[:, :], 0.0).then_inc(s_zset, 1)
            pool.wait_ge(s_mom, TILES)
            pool.tensor_tensor(vareps[:, :], mv[:, :, 1], consts["ln_eps"][:, :], ALU.add).then_inc(s_veps, 1)
            pool.wait_ge(s_veps, 1)
            pool.tensor_tensor(rstd[:, :], vareps[:, :], consts["mhalf"][:, :], ALU.pow).then_inc(s_rstd, 1)
            pool.wait_ge(s_zero, 16 * ZDMAS)
            pool.wait_ge(s_h, TILES)
            pool.wait_ge(s_slot, 1)
            for k in range(top):
                for T in range(TILES):
                    pool.indirect_dma_start(out=xs_rows, out_offset=bass.IndirectOffsetOnAxis(ap=slot_u[:, k, T:T + 1], axis=0),
                                            in_=h[:, T, :], in_offset=None).then_inc(s_sc, 16)
            pool.wait_ge(s_sc, 16 * top * TILES)

        @block.vector
        def _(dve):
            steps = [0]

            def step(ins):
                steps[0] += 1
                ins.then_inc(s_dv, 1)
                dve.wait_ge(s_dv, steps[0])

            for T in range(TILES):
                last = dve.bn_stats(stats[:, T, :], x[:, T, :])
                if T == TILES - 1:
                    step(last)
            for T in range(TILES):
                dve.bn_aggr(mv[:, T, :], stats[:, T, :]).then_inc(s_mom, 1)
            dve.memset(ones[:, :], 1.0).then_inc(s_const, 1)
            dve.wait_ge(s_load, LOADED)
            dve.tensor_copy(prefix[:, :], prefix_f[:, :]).then_inc(s_const, 1)
            dve.wait_ge(s_rstd, 1)
            for T in range(TILES):
                dve.tensor_scalar(h[:, T, :], x[:, T, :], mv[:, T, 0:1], rstd[:, T:T + 1], ALU.subtract, ALU.mult)\
                   .then_inc(s_h, 1)
            dve.wait_ge(s_lg, 1)
            lg = LG[:, 0:TILES * E].rearrange("p (t e) -> p t e", e=E)
            if "router_b" in w:
                step(dve.tensor_tensor(logits[:, :, :], lg, rbias[:, :].unsqueeze(1).broadcast_to([P, TILES, E]), ALU.add))
            else:
                step(dve.tensor_copy(logits[:, :, :], lg))
            for T in range(TILES):
                last = dve.max(best[:, T, :], logits[:, T, :])
            step(last)
            for T in range(TILES):
                last = dve.max_index(best_i[:, T, :], best[:, T, :], logits[:, T, :])
            step(last)
            if top == 2:
                dve.tensor_tensor(margin[:, :], best[:, :, 0], best[:, :, 1], ALU.subtract).then_inc(s_mg, 1)
            step(dve.tensor_copy(best_f[:, :, :], best_i[:, :, :]))
            io = iota[:, 0:E].unsqueeze(1).broadcast_to([P, TILES, E])
            for k in range(top):
                last = dve.tensor_tensor(one_hot[:, k, :, :], io, best_f[:, :, k:k + 1].broadcast_to([P, TILES, E]),
                                         ALU.is_equal)
            step(last)
            if top == 2:
                dve.tensor_tensor(chosen[:, :, :], one_hot[:, 0, :, :], one_hot[:, 1, :, :], ALU.add).then_inc(s_ch, 1)
            else:
                dve.tensor_copy(chosen[:, :, :], one_hot[:, 0, :, :]).then_inc(s_ch, 1)
            dve.wait_ge(s_cn, 1)
            step(dve.tensor_scalar(counts[:, :], CN[:, 0:E], 1.0 / GR, None, ALU.mult))
            step(dve.tensor_tensor(filled[:, :, :], counts[:, :].unsqueeze(2).broadcast_to([P, E, MOST]),
                                   iota[:, 0:MOST].unsqueeze(1).broadcast_to([P, E, MOST]), ALU.is_gt))
            step(dve.reduce_sum(groups[:, :], filled[:, :, :], AXX))
            step(dve.tensor_copy(upto[0][:, :], groups[:, :]))
            for n, by in enumerate((1, 2, 4)):
                dve.tensor_copy(upto[n + 1][:, 0:by], upto[n][:, 0:by])
                step(dve.tensor_tensor(upto[n + 1][:, by:E], upto[n][:, by:E], upto[n][:, 0:E - by], ALU.add))
            last_group = upto[3]
            step(dve.tensor_tensor(base[:, :], last_group[:, :], groups[:, :], ALU.subtract))
            step(dve.tensor_scalar(base[:, :], base[:, :], float(GR), None, ALU.mult))
            step(dve.tensor_tensor(passed[:, :, :], last_group[:, :].unsqueeze(1).broadcast_to([P, GROUPS, E]),
                                   iota[:, 0:GROUPS].unsqueeze(2).broadcast_to([P, GROUPS, E]), ALU.is_le))
            step(dve.reduce_sum(expert_f[:, :], passed[:, :, :], AXX))
            step(dve.tensor_scalar(expert_c[:, :], expert_f[:, :], float(E - 1), None, ALU.min))
            step(dve.tensor_copy(expert_i[:, :], expert_c[:, :]))
            dve.wait_ge(s_rk, 1)
            step(dve.tensor_tensor(place[:, :, :], RK[:, 0:TILES * E].rearrange("p (t e) -> p t e", e=E),
                                   base[:, :].unsqueeze(1).broadcast_to([P, TILES, E]), ALU.add))
            for k in range(top):
                step(dve.tensor_tensor(picked[:, k, :, :], place[:, :, :], one_hot[:, k, :, :], ALU.mult))
                step(dve.reduce_sum(slot_f[:, k, :], picked[:, k, :, :], AXX))
            dve.tensor_copy(slot_u[:, :, :], slot_f[:, :, :]).then_inc(s_slot, 1)

        @block.scalar
        def _(act):
            for u in range(TILES // 2):
                act.wait_ge(s_tr, u + 1)
                act.activation(hT[:, :, u * SEQ:(u + 1) * SEQ], TB[u % 4][:, :].rearrange("p (d s) -> p d s", d=DT), ACT.Copy)\
                   .then_inc(s_tc, 1)
            if top == 2:
                act.wait_ge(s_mg, 1)
                act.activation(weight[:, 0, :], margin[:, :], ACT.Sigmoid).then_inc(s_wt, 1)
                act.activation(weight[:, 1, :], margin[:, :], ACT.Sigmoid, scale=-1.0).then_inc(s_wt, 1)

        @block.tensor
        def _(pe):
            for u in range(TILES // 2):
                pe.wait_ge(s_h, 2 * u + 2)
                if u >= 4:
                    pe.wait_ge(s_tc, u - 3)
                for d in range(DT):
                    for t in range(TT):
                        c = d * SEQ + t * P
                        last = pe.transpose(TB[u % 4][:, c:c + P], h[:, 2 * u + t, d * P:(d + 1) * P], ident[:, :])
                last.then_inc(s_tr, 1)
            pe.wait_ge(s_load, LOADED)
            for T in range(TILES):
                pe.wait_ge(s_tc, T // 2 + 1)
                for kk in range(DT):
                    last = pe.matmul(LG[:, T * E:(T + 1) * E], hT[:, kk, T * P:(T + 1) * P], router[:, kk, :],
                                     start=(kk == 0), stop=(kk == DT - 1))
            last.then_inc(s_lg, 1)
            pe.wait_ge(s_const, 2)
            pe.wait_ge(s_ch, 1)
            for T in range(TILES):
                last = pe.matmul(CN[:, 0:E], ones[:, :], chosen[:, T, :], start=(T == 0), stop=(T == TILES - 1))
            last.then_inc(s_cn, 1)
            ch = chosen[:, :, :].rearrange("p t e -> p (t e)")
            W = TILES * E
            pe.matmul(RK[:, 0:W], prefix[:, :], ch, start=True, stop=False, skip_group_check=True)
            for d in range(1, TILES):
                last = pe.matmul(RK[:, d * E:W], ones[:, :], ch[:, 0:W - d * E], start=False, stop=(d == TILES - 1),
                                 skip_group_check=True)
            last.then_inc(s_rk, 1)


def combine_rows(nc, name, x, top, ys_rows, slot_u, weight):
    QUARTERS = 4
    with ExitStack() as ctx:
        sc = Scope(nc, ctx, name + "c")
        got = sc.sb("got", [P, top, TILES, DM])
        s_got = [sc.sem(f"got{n}") for n in range(QUARTERS)]
        s_sum = sc.sem("sum")
        PER = TILES // QUARTERS
        block = ctx.enter_context(nc.Block())

        @block.gpsimd
        def _(pool):
            for T in range(TILES):
                for k in range(top):
                    pool.indirect_dma_start(out=got[:, k, T, :], out_offset=None, in_=ys_rows,
                                            in_offset=bass.IndirectOffsetOnAxis(ap=slot_u[:, k, T:T + 1], axis=0))\
                        .then_inc(s_got[T // PER], 16)

        @block.vector
        def _(dve):
            for T in range(TILES):
                dve.wait_ge(s_got[T // PER], 16 * top * PER)
                if top == 1:
                    dve.tensor_tensor(x[:, T, :], got[:, 0, T, :], x[:, T, :], ALU.add).then_inc(s_sum, 1)
                else:
                    for k in range(top):
                        if k:
                            dve.wait_ge(s_sum, T * top + k)
                        dve.scalar_tensor_tensor(x[:, T, :], got[:, k, T, :], weight[:, k, T:T + 1], x[:, T, :],
                                                 ALU.mult, ALU.add).then_inc(s_sum, 1)
            dve.wait_ge(s_sum, TILES * top)


def build(nc, t, out):
    Scope.taken.clear()
    with ExitStack() as ctx:
        x = ctx.enter_context(nc.sbuf_tensor("x", [P, TILES, DM], F32))
        consts = {"ident": ctx.enter_context(nc.sbuf_tensor("ident", [P, P], F32)),
                  "ident_bf": ctx.enter_context(nc.sbuf_tensor("ident_bf", [P, P], BF16)),
                  "mhalf": ctx.enter_context(nc.sbuf_tensor("mhalf", [P, TILES], F32)),
                  "parity": ctx.enter_context(nc.sbuf_tensor("parity", [P, 2], F32)),
                  "ln_eps": ctx.enter_context(nc.sbuf_tensor("ln_eps", [P, TILES], F32)),
                  "ret_eps": ctx.enter_context(nc.sbuf_tensor("ret_eps", [P, TILES], F32))}
        retention_layer(nc, "ret", x, consts, {
            "x": t["x"], "wq": t["L0_attn_Wq"], "wk": t["L0_attn_Wk"], "wv": t["L0_attn_Wv"], "wg": t["L0_attn_Wg"],
            "wo": t["L0_attn_Wo"], "bo": t["L0_attn_bo"], "bg": t["L0_attn_bg"], "gamma": t["L0_attn_ln_gamma"],
            "beta": t["L0_attn_ln_beta"], "qdec": t["qdec"], "kdec": t["kdec"], "keep": t["keep"],
            "ident": t["ident"], "mhalf": t["mhalf"], "ln_eps": t["ln_eps"], "parity": t["parity"], "ret_eps": t["ret_eps"]})
        if STAGES >= 2:
            bf16_identity(nc, consts)
            attention_layer(nc, "x0", x, consts, {
                "wq": t["L0_xattn_Wq"], "wk": t["L0_xattn_Wk"], "wv": t["L0_xattn_Wv"], "wo": t["L0_xattn_Wo"],
                "bq": t["L0_xattn_bq"], "bk": t["L0_xattn_bk"], "bv": t["L0_xattn_bv"], "bo": t["L0_xattn_bo"],
                "ctxT": t["ctxT"], "mask": t["mask"]}, dh=16, cross=True, masked=True, causal=False)
        if STAGES >= 3:
            expert_layer(nc, "e0", x, consts, {
                "router": t["L0_ffn_router_w"], "router_b": t["L0_ffn_router_b"], "w1": t["L0_ffn_w1"],
                "b1": t["L0_ffn_b1"], "w2": t["L0_ffn_w2"], "b2": t["L0_ffn_b2"], "prefix": t["prefix"],
                "iota": t["iota"]}, top=1, hidden=1024)
            Scope.clear_semaphores(nc)
        if STAGES >= 4:
            attention_layer(nc, "a1", x, consts, {
                "wq": t["L1_attn_Wq"], "wk": t["L1_attn_Wk"], "wv": t["L1_attn_Wv"], "wo": t["L1_attn_Wo"],
                "bo": t["L1_attn_bo"], "cosx": t["cosx"], "sinx": t["sinx"], "causal": t["causal"]},
                dh=64, cross=False, masked=False, causal=True)
        if STAGES >= 5:
            attention_layer(nc, "x1", x, consts, {
                "wq": t["L1_xattn_w_q"], "wk": t["L1_xattn_w_k"], "wv": t["L1_xattn_w_v"], "wo": t["L1_xattn_w_o"],
                "bq": t["L1_xattn_b_q"], "bk": t["L1_xattn_b_k"], "bv": t["L1_xattn_b_v"], "bo": t["L1_xattn_b_o"],
                "ctxT": t["ctxT"]}, dh=16, cross=True, masked=False, causal=False)
        if STAGES >= 6:
            expert_layer(nc, "e1", x, consts, {
                "router": t["L1_ffn_router_w"], "gate": t["L1_ffn_gate_proj"], "up": t["L1_ffn_up_proj"],
                "down": t["L1_ffn_down_proj"], "prefix": t["prefix"], "iota": t["iota"]}, top=2, hidden=704)
        s_store = ctx.enter_context(nc.semaphore("store"))
        with nc.Block() as block:
            @block.sync
            def _(sp):
                sp.dma_start(out.rearrange("b (t p) n -> p (b t) n", p=P), x[:, :, :]).then_inc(s_store, 16)
                sp.wait_ge(s_store, 16)


def bf16_identity(nc, consts):
    with nc.semaphore("identbf") as s_id, nc.Block() as block:
        @block.vector
        def _(dve):
            dve.tensor_copy(consts["ident_bf"][:, :], consts["ident"][:, :]).then_inc(s_id, 1)
            dve.wait_ge(s_id, 1)



def kernel(**inputs):
    import numpy as np
    import concourse.bacc as bacc
    from concourse.bass_utils import run_bass_kernel_spmd as run

    nc = bacc.Bacc("TRN2", target_bir_lowering=False, num_devices=1)
    arrays = {}

    def cols(b):
        return np.asarray(b).reshape(-1, P).T

    def cols_by_parity(b):
        c = np.asarray(b).reshape(-1, P // 32, 2, 16)
        out = np.zeros((2,) + c.shape, c.dtype)
        for e in range(2):
            out[e, :, :, e] = c[:, :, e]
        return out.reshape(2, -1, P).transpose(2, 1, 0)

    for k, v in inputs.items():
        v = np.asarray(v)
        if k in ("L1_xattn_w_q", "L1_xattn_w_k", "L1_xattn_w_v", "L1_xattn_w_o"):
            v = v.T
        elif k in ("L0_xattn_bq", "L1_xattn_b_q", "L0_xattn_bv", "L1_xattn_b_v"):
            v = cols(v)
        elif k in ("L0_xattn_bk", "L1_xattn_b_k"):
            v = cols_by_parity(v)
        elif k == "L0_ffn_b1":
            v = v.reshape(8, -1, P).transpose(0, 2, 1)
        elif k == "mask_SxS2_bk1":
            k = "mask"
        elif k == "ctx_1024":
            k, v = "ctxT", v.transpose(2, 0, 1).reshape(DM, BATCH * SEQ)
        arrays[k] = np.ascontiguousarray(v)

    arrays["ident"] = np.eye(P, dtype=np.float32)
    arrays["mhalf"] = np.full((P, TILES), -0.5, np.float32)
    arrays["ln_eps"] = np.full((P, TILES), LN_EPS, np.float32)
    arrays["ret_eps"] = np.full((P, TILES), RET_EPS, np.float32)
    gam = 1.0 - 2.0 ** (-5.0 - np.arange(HEADS, dtype=np.float64))
    tpos = np.arange(SEQ, dtype=np.float64)
    qd = (gam[:, None] ** tpos[None, :]) * 0.25
    kd = gam[:, None] ** (-tpos[None, :])
    head_of = 8 * np.arange(DT)[None, :] + (np.arange(P) // 16)[:, None]
    parity = np.stack([(np.arange(P) // 16) % 2 == e for e in range(2)], 1).astype(np.float32)
    arrays["parity"] = parity
    arrays["qdec"] = qd[head_of].astype(np.float32)
    arrays["kdec"] = (kd[head_of][:, None] * parity[:, :, None, None]).astype(np.float32)
    tri = (np.arange(P)[None, :] >= np.arange(P)[:, None]).astype(np.float32)
    arrays["keep"] = np.concatenate([tri, np.ones((P, P), np.float32), tri], 1)
    late = np.where(np.arange(SEQ)[None, None, :] > (np.arange(P)[:, None, None] + P * np.arange(TT)[None, :, None]), NEG, 0.0)
    arrays["causal"] = late.astype(np.float32)
    inv = (1.0 / np.float32(10000.0) ** (np.arange(0, 64, 2, dtype=np.float32) / np.float32(64))).astype(np.float32)
    ang = (np.arange(SEQ, dtype=np.float32)[:, None] * inv[None, :]).astype(np.float32)
    cos = np.cos(ang.astype(np.float64)).reshape(TT, P, 32).transpose(1, 0, 2)
    sin = np.sin(ang.astype(np.float64)).reshape(TT, P, 32).transpose(1, 0, 2)
    c2 = np.repeat(cos, 2, axis=-1)
    s2 = np.concatenate([-sin, sin], -1)
    arrays["cosx"] = np.stack([c2 * 0.125, c2], 1).astype(np.float32)
    arrays["sinx"] = np.stack([s2 * 0.125, s2], 1).astype(np.float32)
    arrays["prefix"] = (np.arange(P)[:, None] < np.arange(P)[None, :]).astype(np.float32)
    arrays["iota"] = np.broadcast_to(np.arange(32, dtype=np.float32), (P, 32)).copy()

    t = {n: nc.dram_tensor(f"in_{n}", a.shape, mybir.dt.from_np(a.dtype), kind="ExternalInput").ap()
         for n, a in arrays.items()}
    out = nc.dram_tensor("out_0", (BATCH, SEQ, DM), F32, kind="ExternalOutput").ap()
    build(nc, t, out)
    r = run(nc, [{f"in_{n}": a for n, a in arrays.items()}], core_ids=[0])
    return r.results[0]["out_0"]
```
